# Optimizing a Trainium2 kernel written in Bass

```python
import numpy as np
import jax
import jax.numpy as jnp

def _softmax(x, axis=-1):
    return jax.nn.softmax(x, axis=axis)

def _gelu(x):
    return jax.nn.gelu(x, approximate=True)

def _silu(x):
    return jax.nn.silu(x)

def _sigmoid(x):
    return jax.nn.sigmoid(x)

def _layernorm(x, axis=-1, eps=1e-05):
    m = jnp.mean(x, axis=axis, keepdims=True)
    v = jnp.var(x, axis=axis, keepdims=True)
    return (x - m) / jnp.sqrt(v + eps)

def _scatter_add(tgt, idx, src, axis=0):
    return tgt.at[idx].add(src)

def _segment_sum(src, seg, n):
    return jax.ops.segment_sum(src, seg, n)
kernel_name = 'mk_decoder_preln_d1_seqx_r8_1812f3'

def setup_inputs(seed: int=0):
    np.random.seed(seed)
    _w = jnp.asarray

    def _rec_inputs():
        import jax
        import jax.numpy as jnp
        _rk = jax.random.key(seed)
        x = -0.0003929 + 0.9999 * jax.random.normal(jax.random.fold_in(_rk, 1), (8, 128, 512), jnp.float32)
        _lenS = 128 - jax.random.randint(jax.random.fold_in(_rk, 7), (8,), 0, max(1, 128 // 4) + 1, jnp.int32)
        _lenS2 = 128 - jax.random.randint(jax.random.fold_in(_rk, 8), (8,), 0, max(1, 128 // 4) + 1, jnp.int32)
        _ctx_4096P = jax.random.normal(jax.random.fold_in(_rk, 11), (8, 16, 512), jnp.float32)
        _ctx_4096c = jax.random.dirichlet(jax.random.fold_in(_rk, 511), 0.3 * jnp.ones((16,), jnp.float32), (8, 128))
        _ctx_4096t = jnp.einsum('bsk,bkd->bsd', _ctx_4096c, _ctx_4096P)
        _ctx_4096t = _ctx_4096t * jax.lax.rsqrt(jnp.mean(jnp.square(_ctx_4096t)) + 1e-12) * 0.953939
        ctx_4096 = 2.81802e-05 + 1.00001 * (_ctx_4096t + 0.3 * jax.random.normal(jax.random.fold_in(_rk, 611), (8, 128, 512), jnp.float32))
        pos_BxS2 = jnp.broadcast_to(jnp.arange(128, dtype=jnp.int32), (8, 128))
        _validS = jnp.arange(128)[None, :] < _lenS[:, None]
        _validS2 = jnp.arange(128)[None, :] < _lenS2[:, None]
        _causal = jnp.tril(jnp.ones((128, 128), dtype=bool))
        mask_BxSxS2_ik0 = jnp.where(jnp.broadcast_to(_validS2[:, None, :], (8, 128, 128)), 0, 1).astype(jnp.int32)
        return (x, ctx_4096, pos_BxS2, mask_BxSxS2_ik0)
    x, ctx_4096, pos_BxS2, mask_BxSxS2_ik0 = _rec_inputs()

    def _L0_attn_setup():
        import jax, jax.numpy as jnp
        import numpy as np
        import math
        B, T, D_IN, D_OUT = (2, 256, 512, 512)
        N_HEADS, N_KV = (32, 8)
        HEAD_DIM = D_OUT // N_HEADS
        GROUP_SIZE = N_HEADS // N_KV
        ROPE_BASE = 500000.0
        CTX = 256

        def _rope_tables(head_dim, base, seq_len):
            inv_freq = 1.0 / base ** (jnp.arange(0, head_dim, 2, dtype=jnp.float32) / head_dim)
            t = jnp.arange(seq_len, dtype=jnp.float32)
            freqs = jnp.einsum('i,j->ij', t, inv_freq)
            return (jnp.cos(freqs), jnp.sin(freqs))

        def _apply_rope(x, cos, sin):
            x1, x2 = jnp.split(x, 2, axis=-1)
            c = cos[None, None]
            s = sin[None, None]
            return jnp.concatenate([x1 * c - x2 * s, x1 * s + x2 * c], axis=-1)
        key = jax.random.key(seed)
        ks = jax.random.split(key, 5)
        scale = 0.02
        return {'x': jax.random.normal(ks[0], (B, T, D_IN), dtype=jnp.float32), 'Wq': jax.random.normal(ks[1], (D_IN, D_OUT), dtype=jnp.float32) * scale, 'Wk': jax.random.normal(ks[2], (D_IN, N_KV * HEAD_DIM), dtype=jnp.float32) * scale, 'Wv': jax.random.normal(ks[3], (D_IN, N_KV * HEAD_DIM), dtype=jnp.float32) * scale, 'Wo': jax.random.normal(ks[4], (D_OUT, D_OUT), dtype=jnp.float32) * scale}
    _L0_attn_all = _L0_attn_setup()
    _L0_attn_in = {k: v for k, v in _L0_attn_all.items() if k in ('Wq', 'Wk', 'Wv', 'Wo')}
    del _L0_attn_all

    def _L0_xattn_setup():
        import jax, jax.numpy as jnp
        import numpy as np
        B, S, E = (2, 256, 512)
        H, KVH, D = (32, 8, 128)
        GROUPS = H // KVH
        MAX_POS = 512
        ROPE_THETA = 10000.0

        def _rope_tables(max_pos, dim, theta):
            inv_freq = 1.0 / theta ** (jnp.arange(0, dim, 2, dtype=jnp.float32) / dim)
            t = jnp.arange(max_pos, dtype=jnp.float32)
            freqs = jnp.einsum('i,j->ij', t, inv_freq)
            emb = jnp.concatenate([freqs, freqs], axis=-1)
            return (jnp.cos(emb), jnp.sin(emb))

        def _rotate_half(x):
            x1, x2 = (x[..., :x.shape[-1] // 2], x[..., x.shape[-1] // 2:])
            return jnp.concatenate([-x2, x1], axis=-1)
        key = jax.random.key(seed)
        ks = jax.random.split(key, 8)
        scale_w = 1.0 / np.sqrt(E)
        query = jax.random.normal(ks[0], (B, S, E), dtype=jnp.float32)
        k_in = jax.random.normal(ks[1], (B, S, E), dtype=jnp.float32)
        v_in = jax.random.normal(ks[2], (B, S, E), dtype=jnp.float32)
        position_ids = jnp.broadcast_to(jnp.arange(S, dtype=jnp.int64), (B, S))
        src_mask = jnp.tril(jnp.ones((S, S), dtype=jnp.int32))
        src_mask = jnp.broadcast_to(src_mask, (B, S, S))
        Wq = jax.random.normal(ks[3], (E, H * D), dtype=jnp.float32) * scale_w
        Wk = jax.random.normal(ks[4], (E, KVH * D), dtype=jnp.float32) * scale_w
        Wv = jax.random.normal(ks[5], (E, KVH * D), dtype=jnp.float32) * scale_w
        Wo = jax.random.normal(ks[6], (H * D, E), dtype=jnp.float32) * scale_w
        return {'query': query, 'key': k_in, 'value': v_in, 'position_ids': position_ids, 'src_mask': src_mask, 'Wq': Wq, 'Wk': Wk, 'Wv': Wv, 'Wo': Wo}
    _L0_xattn_all = _L0_xattn_setup()
    _L0_xattn_in = {k: v for k, v in _L0_xattn_all.items() if k in ('Wq', 'Wk', 'Wv', 'Wo')}
    del _L0_xattn_all

    def _L0_ffn_setup():
        import jax, jax.numpy as jnp
        import numpy as np
        K_TOP = 8
        key = jax.random.key(seed)
        k1, k2, k3 = jax.random.split(key, 3)
        B, S, H, E = (4, 512, 512, 64)
        hidden_states = jax.random.normal(k1, (B, S, H), dtype=jnp.float32)
        router_weight = jax.random.normal(k2, (E, H), dtype=jnp.float32)
        router_bias = jnp.zeros((E,), dtype=jnp.float32)
        expert_bias = jax.random.normal(k3, (E, H), dtype=jnp.float32) * 0.1
        return {'hidden_states': hidden_states, 'router_weight': router_weight, 'router_bias': router_bias, 'expert_bias': expert_bias}
    _L0_ffn_all = _L0_ffn_setup()
    _L0_ffn_in = {k: v for k, v in _L0_ffn_all.items() if k in ('router_weight', 'router_bias', 'expert_bias')}
    del _L0_ffn_all
    return {'x': x, 'ctx_4096': ctx_4096, 'pos_BxS2': pos_BxS2, 'mask_BxSxS2_ik0': mask_BxSxS2_ik0, 'L0_attn_Wq': _L0_attn_in['Wq'], 'L0_attn_Wk': _L0_attn_in['Wk'], 'L0_attn_Wv': _L0_attn_in['Wv'], 'L0_attn_Wo': _L0_attn_in['Wo'], 'L0_xattn_Wq': _L0_xattn_in['Wq'], 'L0_xattn_Wk': _L0_xattn_in['Wk'], 'L0_xattn_Wv': _L0_xattn_in['Wv'], 'L0_xattn_Wo': _L0_xattn_in['Wo'], 'L0_ffn_router_weight': _L0_ffn_in['router_weight'], 'L0_ffn_router_bias': _L0_ffn_in['router_bias'], 'L0_ffn_expert_bias': _L0_ffn_in['expert_bias']}

def reference(x, ctx_4096, pos_BxS2, mask_BxSxS2_ik0, L0_attn_Wq, L0_attn_Wk, L0_attn_Wv, L0_attn_Wo, L0_xattn_Wq, L0_xattn_Wk, L0_xattn_Wv, L0_xattn_Wo, L0_ffn_router_weight, L0_ffn_router_bias, L0_ffn_expert_bias):
    import jax
    import jax.numpy as jnp

    def _L0_attn_ref(x, Wq, Wk, Wv, Wo):
        import jax, jax.numpy as jnp
        import numpy as np
        import math
        B, T, D_IN, D_OUT = (2, 256, 512, 512)
        N_HEADS, N_KV = (32, 8)
        HEAD_DIM = D_OUT // N_HEADS
        GROUP_SIZE = N_HEADS // N_KV
        ROPE_BASE = 500000.0
        CTX = 256

        def _rope_tables(head_dim, base, seq_len):
            inv_freq = 1.0 / base ** (jnp.arange(0, head_dim, 2, dtype=jnp.float32) / head_dim)
            t = jnp.arange(seq_len, dtype=jnp.float32)
            freqs = jnp.einsum('i,j->ij', t, inv_freq)
            return (jnp.cos(freqs), jnp.sin(freqs))

        def _apply_rope(x, cos, sin):
            x1, x2 = jnp.split(x, 2, axis=-1)
            c = cos[None, None]
            s = sin[None, None]
            return jnp.concatenate([x1 * c - x2 * s, x1 * s + x2 * c], axis=-1)
        b, t, _ = x.shape
        cos, sin = _rope_tables(HEAD_DIM, ROPE_BASE, t)
        q = (x @ Wq).reshape(b, t, N_HEADS, HEAD_DIM).transpose(0, 2, 1, 3)
        k = (x @ Wk).reshape(b, t, N_KV, HEAD_DIM).transpose(0, 2, 1, 3)
        v = (x @ Wv).reshape(b, t, N_KV, HEAD_DIM).transpose(0, 2, 1, 3)
        q = _apply_rope(q, cos, sin)
        k = _apply_rope(k, cos, sin)
        k_h = jnp.repeat(k, GROUP_SIZE, axis=1)
        v_h = jnp.repeat(v, GROUP_SIZE, axis=1)
        scores = jnp.einsum('bhqd,bhkd->bhqk', q, k_h) / math.sqrt(HEAD_DIM)
        causal = jnp.triu(jnp.ones((t, t), dtype=bool), k=1)
        scores = jnp.where(causal[None, None], jnp.finfo(scores.dtype).min, scores)
        attn = jax.nn.softmax(scores, axis=-1)
        ctx = jnp.einsum('bhqk,bhkd->bhqd', attn, v_h)
        ctx = ctx.transpose(0, 2, 1, 3).reshape(b, t, D_OUT)
        return ctx @ Wo

    def _L0_xattn_ref(query, key, value, position_ids, src_mask, Wq, Wk, Wv, Wo):
        import jax, jax.numpy as jnp
        import numpy as np
        B, S, E = (2, 256, 512)
        H, KVH, D = (32, 8, 128)
        GROUPS = H // KVH
        MAX_POS = 512
        ROPE_THETA = 10000.0

        def _rope_tables(max_pos, dim, theta):
            inv_freq = 1.0 / theta ** (jnp.arange(0, dim, 2, dtype=jnp.float32) / dim)
            t = jnp.arange(max_pos, dtype=jnp.float32)
            freqs = jnp.einsum('i,j->ij', t, inv_freq)
            emb = jnp.concatenate([freqs, freqs], axis=-1)
            return (jnp.cos(emb), jnp.sin(emb))

        def _rotate_half(x):
            x1, x2 = (x[..., :x.shape[-1] // 2], x[..., x.shape[-1] // 2:])
            return jnp.concatenate([-x2, x1], axis=-1)
        nb, q_len, _ = query.shape
        q = (query @ Wq).reshape(nb, q_len, H, D).transpose(0, 2, 1, 3)
        k = (key @ Wk).reshape(nb, q_len, KVH, D).transpose(0, 2, 1, 3)
        v = (value @ Wv).reshape(nb, q_len, KVH, D).transpose(0, 2, 1, 3)
        cos_t, sin_t = _rope_tables(MAX_POS, D, ROPE_THETA)
        cos = cos_t[position_ids][:, None]
        sin = sin_t[position_ids][:, None]
        q = q * cos + _rotate_half(q) * sin
        k = k * cos + _rotate_half(k) * sin
        k = jnp.repeat(k, GROUPS, axis=1)
        v = jnp.repeat(v, GROUPS, axis=1)
        scores = jnp.einsum('bhqd,bhkd->bhqk', q, k) / jnp.sqrt(jnp.float32(D))
        mask = src_mask[:, None]
        scores = jnp.where(mask == 0, jnp.float32(-1000000000.0), scores)
        attn = jax.nn.softmax(scores, axis=-1)
        x = jnp.einsum('bhqk,bhkd->bhqd', attn, v)
        x = x.transpose(0, 2, 1, 3).reshape(nb, q_len, H * D)
        return x @ Wo

    def _L0_ffn_ref(hidden_states, router_weight, router_bias, expert_bias):
        import jax, jax.numpy as jnp
        import numpy as np
        K_TOP = 8
        B, S, H = hidden_states.shape
        E = router_weight.shape[0]
        T = B * S
        flat = hidden_states.reshape(T, H)
        logits = jnp.einsum('th,eh->te', flat, router_weight) + router_bias
        scores = jax.nn.softmax(logits, axis=-1)
        topk_w, topk_idx = jax.lax.top_k(scores, K_TOP)
        w_sum = topk_w.sum(axis=-1, keepdims=True)
        w_dense = jnp.zeros((T, E), dtype=scores.dtype).at[jnp.arange(T)[:, None], topk_idx].add(topk_w)
        bias_mix = jnp.einsum('te,eh->th', w_dense, expert_bias)
        out = flat * w_sum + bias_mix
        return out.reshape(B, S, H)
    x = x + _L0_attn_ref(_layernorm(x, axis=-1), L0_attn_Wq, L0_attn_Wk, L0_attn_Wv, L0_attn_Wo)
    x = x + _L0_xattn_ref(_layernorm(x, axis=-1), ctx_4096, ctx_4096, pos_BxS2, mask_BxSxS2_ik0, L0_xattn_Wq, L0_xattn_Wk, L0_xattn_Wv, L0_xattn_Wo)
    x = x + _L0_ffn_ref(_layernorm(x, axis=-1), L0_ffn_router_weight, L0_ffn_router_bias, L0_ffn_expert_bias)
    return x

_drawn_inputs = setup_inputs


def setup_inputs(seed=0):
    import zlib

    import numpy as np

    out = dict(_drawn_inputs(seed))
    spreads = {'L0_ffn_router_bias': (0.0, 0.8)}
    factors = {'L0_attn_Wq': 8.0, 'L0_attn_Wk': 8.0}
    for name, (base, spread) in spreads.items():
        noise = np.random.default_rng([zlib.crc32(name.encode()), seed]).standard_normal(out[name].shape)
        drawn = base * np.exp(spread * noise) if base else spread * noise
        out[name] = jnp.asarray(drawn.astype(out[name].dtype))
    for name, factor in factors.items():
        out[name] = (out[name] * factor).astype(out[name].dtype)
    return out
```

```python
from contextlib import ExitStack
import math

import concourse.bass as bass
from concourse import mybir

F32 = mybir.dt.float32
I32 = mybir.dt.int32
U32 = mybir.dt.uint32
ALU = mybir.AluOpType
ACT = mybir.ActivationFunctionType
AX = mybir.AxisListType

P = 128
NB = 8
E = 512
EC = E // P
NU = 8
UH = 4
NG = 8
GH = 4
SD = 16
XD = 128
MAXPOS = 512
SELF_SCALE = 1.0 / math.sqrt(SD)
CROSS_SCALE = 1.0 / math.sqrt(XD)
NEG = -float(2 ** 100)
BIG = 3.0e38
EPS = 1e-5
NE = 64
TOP = 8
VZ = 9 * SD
HALF_TOK = 4 * P


def decoder(nc, x, ctx, pos, mask, wq_s, wk_s, wv_s, wo_s, wq_x, wk_x, wv_x, wo_x,
            router_w, router_b, expert_b, c_ident, c_causal, c_rope_self, c_rope_cross, c_rows, out):
    k_dram = nc.dram_tensor("k_cross", (NG, XD, NB * P), F32, kind="Internal").ap()
    v_dram = nc.dram_tensor("v_cross", (NB, P, NG * XD), F32, kind="Internal").ap()

    with ExitStack() as whole:
        def sem(name):
            return whole.enter_context(nc.semaphore(name))

        def keep(name, shape, dt=F32):
            return whole.enter_context(nc.sbuf_tensor(name, shape, dt))

        bank = [whole.enter_context(nc.psum_tensor(f"bank{i}", [P, 512], F32)) for i in range(8)]

        ident = keep("ident", [P, P])
        X = keep("X", [P, NB, E])
        rope_x = keep("rope_x", [P, NB, 4 * 64])
        mean_var = keep("mean_var", [P, NB, 2])
        stats = keep("stats", [P, 6])
        one_row = keep("one_row", [P, 2])
        spread = keep("spread", [P, NB])
        rstd = keep("rstd", [P, NB])
        eps = keep("eps", [P, 1])
        neg_scores = keep("neg_scores", [P, 2, UH, P])
        neg_max = keep("neg_max", [P, 2, UH])
        exps = keep("exps", [P, 2, UH, P])
        sums = keep("sums", [P, 2, UH])
        rsums = keep("rsums", [P, 2, UH])
        probs = keep("probs", [P, 2, UH, P])
        probsT = keep("probsT", [P, 2, UH, P])
        wq_g = keep("wq_g", [P, GH, EC, XD])
        wo_g = keep("wo_g", [P, 2, GH, E])
        xn2T = keep("xn2T", [P, EC, NB * P])

        first = ExitStack()

        def one(name, shape, dt=F32):
            return first.enter_context(nc.sbuf_tensor(name, shape, dt))

        causal = one("causal", [P, P])
        rope_s = one("rope_s", [P, 2 * SD])
        rows = one("rows", [P, NG])
        wq1 = one("wq1", [P, EC, E])
        wkv1 = one("wkv1", [P, EC, 2 * P])
        wo1 = one("wo1", [P, GH, E])
        wk2 = one("wk2", [P, EC, NG * XD])
        wv2 = one("wv2", [P, EC, NG * XD])
        posf = one("posf", [P, NB])
        posi = one("posi", [P, NB], I32)
        posn = one("posn", [P, NB])
        posu = one("posu", [P, NB], U32)
        xn = one("xn", [P, E])
        xnT = one("xnT", [P, EC, P])
        cx = one("cx", [P, E])
        cxT = one("cxT", [P, EC, P])
        qa = one("qa", [P, E])
        qb = one("qb", [P, E])
        qr = one("qr", [P, E])
        ka = one("ka", [P, P])
        kb = one("kb", [P, P])
        kr = one("kr", [P, P])
        kxa = one("kxa", [P, 2, E])
        kxb = one("kxb", [P, 2, E])
        kxr = one("kxr", [P, 2, E])
        kxT = one("kxT", [P, NG, P])
        vx = one("vx", [P, NG * XD])
        qT = one("qT", [P, GH, P])
        kTz = one("kTz", [P, NG, P])
        vz = one("vz", [P, NG * VZ])
        atT = one("atT", [P, GH, P])
        first.close()

        second = ExitStack()

        def two(name, shape, dt=F32):
            return second.enter_context(nc.sbuf_tensor(name, shape, dt))

        k_g = two("k_g", [P, 2, NB * P])
        v_g = two("v_g", [P, 2, NB, XD])
        Q = two("Q", [P, GH, NB * P])
        cosT = two("cosT", [P, NB * P])
        sinT = two("sinT", [P, NB * P])
        ra = two("ra", [P, 2, HALF_TOK])
        rb = two("rb", [P, 2, HALF_TOK])
        xn2 = two("xn2", [P, 2, E])
        maski = two("maski", [P, NB, P], I32)
        bias = two("bias", [P, NB, P])
        oT = two("oT", [P, GH, P])
        xn3 = two("xn3", [P, NB, E])
        xn3T = two("xn3T", [P, EC, NB * P])
        rw = two("rw", [NE, E])
        rwT = two("rwT", [P, EC, NE])
        rb_row = two("rb_row", [P, NE])
        eb = two("eb", [NE, E])
        lg = two("lg", [P, NB, NE])
        lmax = two("lmax", [P, NB])
        lsum = two("lsum", [P, NB])
        lrs = two("lrs", [P, NB])
        lsh = two("lsh", [P, NB, NE])
        lex = two("lex", [P, NB, NE])
        lsc = two("lsc", [P, NB, NE])
        top = two("top", [P, NB, TOP])
        cut = two("cut", [P, NB, NE])
        wd = two("wd", [P, NB, NE])
        wsum = two("wsum", [P, NB])
        wdT = two("wdT", [NE, NB * P])
        second.close()

        x_in = [sem(f"x_in{b}") for b in range(NB)]
        wq_in = [sem(f"wq_in{j}") for j in range(GH)]
        ident_in, small_in, pos_in = sem("ident_in"), sem("small_in"), sem("pos_in")
        wqkv_in, wkv2_in, wo1_in, ctx_in_ = sem("wqkv_in"), sem("wkv2_in"), sem("wo1_in"), sem("ctx_in")
        gathered, wo_in, kv_in = sem("gathered"), sem("wo_in"), sem("kv_in")
        mask_in, ffn_in, stored, kv_stored = sem("mask_in"), sem("ffn_in"), sem("stored"), sem("kv_stored")
        eps_set, stats_done, aggr_done, mv_done = sem("eps_set"), sem("stats_done"), sem("aggr_done"), sem("mv_done")
        spread_done, rstd_done = sem("spread_done"), sem("rstd_done")
        pos_a, pos_b, pos_ready = sem("pos_a"), sem("pos_b"), sem("pos_ready")
        vz_zero = sem("vz_zero")
        xn_ready, xnT_ps, xnT_ready = sem("xn_ready"), sem("xnT_ps"), sem("xnT_ready")
        cxT_ps, cxT_ready = sem("cxT_ps"), sem("cxT_ready")
        q_ps, kv_ps, kx_ps, vx_ps = sem("q_ps"), sem("kv_ps"), sem("kx_ps"), sem("vx_ps")
        qab_done, qr_ready, kab_done, kr_ready = sem("qab_done"), sem("qr_ready"), sem("kab_done"), sem("kr_ready")
        v_ready, kxab_done, kxr_ready, vx_ready = sem("v_ready"), sem("kxab_done"), sem("kxr_ready"), sem("vx_ready")
        qT_ps, qT_ready, kT_ps, kTz_ready = sem("qT_ps"), sem("qT_ready"), sem("kT_ps"), sem("kTz_ready")
        kxT_ps, kxT_ready = sem("kxT_ps"), sem("kxT_ready")
        at_ready, o_ps, x1_ready = sem("at_ready"), sem("o_ps"), sem("x1_ready")
        s_ready, masked, exp_done, rsum_ready = sem("s_ready"), sem("masked"), sem("exp_done"), sem("rsum_ready")
        prob_ready, pT_ps, pT_ready, av_done = sem("prob_ready"), sem("pT_ps"), sem("pT_ready"), sem("av_done")
        xn2_ready, xn2T_ps, xn2T_ready = sem("xn2_ready"), sem("xn2T_ps"), sem("xn2T_ready")
        tab_ps, tab_ready, bias_ready = sem("tab_ps"), sem("tab_ready"), sem("bias_ready")
        qp_done, rope_ab, q_ready = sem("qp_done"), sem("rope_ab"), sem("q_ready")
        oT_ready, y_done, acc_done = sem("oT_ready"), sem("y_done"), sem("acc_done")
        xn3_ready, xn3T_ps, xn3T_ready = sem("xn3_ready"), sem("xn3T_ps"), sem("xn3T_ready")
        rwT_ps, rwT_ready, lg_ps, ffn_step = sem("rwT_ps"), sem("rwT_ready"), sem("lg_ps"), sem("ffn_step")
        lex_done, wdT_ps, wdT_ready = sem("lex_done"), sem("wdT_ps"), sem("wdT_ready")
        mix_ps, fin_ready = sem("mix_ps"), sem("fin_ready")

        ONE, STORE_ONE = 1, 16
        sp_passed, dve_passed = sem("sp_passed"), sem("dve_passed")

        CROSS0 = NB * NU
        PIECES = [(half, head) for half in range(2) for head in range(GH)]
        LEAD = 6

        def piece_at(slot):
            n = slot + LEAD
            return (0, n) if n < 8 else (1, n - 8)

        def row(t, b):
            return t[:, bass.ds(b, 1), :].rearrange("p o n -> p (o n)")

        block = whole.enter_context(nc.Block())

        @block.sync
        def _(sp):
            sp.sem_inc(kv_stored, STORE_ONE)
            sp.dma_start(ident[:], c_ident).then_inc(ident_in, 16)
            for b in range(NB):
                sp.dma_start(X[:, b, :], x[b]).then_inc(x_in[b], 16)
            sp.dma_start(wq1[:], wq_s.rearrange("(c p) n -> p c n", p=P)).then_inc(wqkv_in, 16)
            sp.dma_start(wkv1[:, :, 0:P], wk_s.rearrange("(c p) n -> p c n", p=P)).then_inc(wqkv_in, 16)
            sp.dma_start(wkv1[:, :, P:2 * P], wv_s.rearrange("(c p) n -> p c n", p=P)).then_inc(wqkv_in, 16)
            sp.dma_start(wk2[:], wk_x.rearrange("(c p) n -> p c n", p=P)).then_inc(wkv2_in, 16)
            sp.dma_start(wv2[:], wv_x.rearrange("(c p) n -> p c n", p=P)).then_inc(wkv2_in, 16)
            for g in range(NG):
                sp.dma_start(wo1[SD * g:SD * (g + 1), :, :],
                             wo_s[g * GH * SD:(g + 1) * GH * SD, :].rearrange("(j d) n -> d j n", d=SD))\
                    .then_inc(wo1_in, 16)
            for j in range(GH):
                sp.dma_start(wq_g[:, j, :, :], wq_x[:, j * XD:(j + 1) * XD].rearrange("(c p) n -> p c n", p=P))\
                    .then_inc(wq_in[j], 16)
            sp.dma_start(wo_g[:, 0, :, :], wo_x[0:GH * XD, :].rearrange("(j p) n -> p j n", p=P))\
                .then_inc(wo_in, 16)
            with sp.Fori(0, NB) as b:
                sp.wait_ge(cxT_ps, ONE + b)
                sp.sem_inc(sp_passed)
                sp.dma_start(cx[:], ctx[bass.ds(b, 1)].rearrange("o p n -> p (o n)")).then_inc(ctx_in_, 16)
                sp.wait_ge(vx_ready, ONE + 2 * b + 2)
                sp.sem_inc(sp_passed)
                sp.dma_start(v_dram[bass.ds(b, 1)].rearrange("o p n -> p (o n)"), vx[:]).then_inc(kv_stored, 16)
                sp.wait_ge(kxT_ready, ONE + 2 * b + 2)
                sp.sem_inc(sp_passed)
                sp.dma_start(k_dram[:, :, bass.ds(b * P, P)].rearrange("g d t -> d g t"), kxT[:])\
                    .then_inc(kv_stored, 16)
            sp.wait_ge(x1_ready, ONE + NB)
            sp.wait_ge(kv_stored, STORE_ONE + 32 * NB)
            sp.dma_start(k_g[:, 0, :], k_dram[0]).then_inc(kv_in, 16)
            sp.dma_start(v_g[:, 0, :, :], v_dram[:, :, 0:XD].rearrange("b k d -> k b d")).then_inc(kv_in, 16)
            sp.dma_start(maski[:], mask.rearrange("b q k -> q b k")).then_inc(mask_in, 16)
            sp.dma_start(rw[:], router_w).then_inc(ffn_in, 16)
            sp.dma_start(eb[:], expert_b).then_inc(ffn_in, 16)
            sp.dma_start(rb_row[:], router_b.rearrange("(o n) -> o n", o=1).to_broadcast([P, NE]))\
                .then_inc(ffn_in, 16)

            def next_group(g, i):
                sp.wait_ge(av_done, ONE + CROSS0 + g * NU)
                sp.sem_inc(sp_passed)
                sp.wait_ge(y_done, ONE + g * NU)
                sp.sem_inc(sp_passed)
                sp.dma_start(k_g[:, 1 - i, :], k_dram[bass.ds(g + 1, 1)].rearrange("o d t -> d (o t)"))\
                    .then_inc(kv_in, 16)
                sp.dma_start(v_g[:, 1 - i, :, :], v_dram[:, :, bass.ds((g + 1) * XD, XD)]
                             .rearrange("b k d -> k b d")).then_inc(kv_in, 16)
                sp.dma_start(wo_g[:, 1 - i, :, :], wo_x[bass.ds((g + 1) * (GH * XD), GH * XD), :]
                             .rearrange("(j p) n -> p j n", p=P)).then_inc(wo_in, 16)
                for j in range(GH):
                    sp.wait_ge(qp_done, ONE + g * 8 + 5 + j)
                    sp.sem_inc(sp_passed)
                    sp.dma_start(wq_g[:, j, :, :], wq_x[:, bass.ds((g + 1) * (GH * XD) + j * XD, XD)]
                                 .rearrange("(c p) n -> p c n", p=P)).then_inc(wq_in[j], 16)

            with sp.Fori(0, NG // 2 - 1) as g2:
                for i in range(2):
                    next_group(g2 * 2 + i, i)
            next_group(NG - 2, 0)
            for b in range(NB):
                sp.wait_ge(fin_ready, b + 1)
                sp.dma_start(out[b], xn3[:, b, :]).then_inc(stored, 16)
            sp.wait_ge(stored, 16 * NB)

        @block.gpsimd
        def _(pool):
            for started in (qr_ready, kxr_ready, prob_ready, q_ready):
                pool.sem_inc(started, ONE)
            pool.dma_start(causal[:], c_causal).then_inc(small_in, 16)
            pool.dma_start(rope_s[:], c_rope_self).then_inc(small_in, 16)
            pool.dma_start(rows[:], c_rows).then_inc(small_in, 16)
            pool.dma_start(posi[:], pos).then_inc(pos_in, 16)
            nc.gpsimd.memset(vz[:], 0.0).then_inc(vz_zero, 1)
            pool.wait_ge(pos_ready, 1)
            for b in range(NB):
                pool.indirect_dma_start(out=rope_x[:, b, :], out_offset=None, in_=c_rope_cross,
                                        in_offset=bass.IndirectOffsetOnAxis(ap=posu[:, b:b + 1], axis=0))\
                    .then_inc(gathered, 16)

            def normalise(i, n, read):
                pool.wait_ge(rsum_ready, ONE + n + 1)
                pool.wait_ge(pT_ps, ONE + read)
                nc.gpsimd.tensor_tensor(probs[:, i], exps[:, i], rsums[:, i].unsqueeze(2).to_broadcast([P, UH, P]),
                                        ALU.mult).then_inc(prob_ready, 1)

            with pool.Fori(0, NB) as b:
                pool.wait_ge(qab_done, ONE + b + 1)
                pool.wait_ge(qT_ps, ONE + b)
                by_group = "p (g j d) -> p g j d"
                nc.gpsimd.tensor_tensor(qr[:].rearrange("p (j g d) -> p g j d", j=GH, g=NG),
                                        qa[:].rearrange(by_group, g=NG, j=GH), qb[:].rearrange(by_group, g=NG, j=GH),
                                        ALU.add).then_inc(qr_ready, 1)
                for i in range(2):
                    pool.wait_ge(kxab_done, ONE + 2 * b + i + 1)
                    pool.wait_ge(kxT_ps, ONE + 2 * b)
                    nc.gpsimd.tensor_tensor(kxr[:, i], kxa[:, i], kxb[:, i], ALU.add).then_inc(kxr_ready, 1)
                for u in range(NU):
                    normalise(u % 2, b * NU + u, b * NU + max(u - 1, 0))

            def rotary_sum(m, half, head, i):
                pool.wait_ge(rope_ab, ONE + m + 1)
                nc.gpsimd.tensor_tensor(Q[:, head, half * HALF_TOK:(half + 1) * HALF_TOK], ra[:, i], rb[:, i],
                                        ALU.add).then_inc(q_ready, 1)

            for m in range(LEAD):
                rotary_sum(m, *PIECES[m], m % 2)
            for u in range(2):
                normalise(u, CROSS0 + u, CROSS0 + u - 1)

            def group(g, last):
                for b in range(NB):
                    n = CROSS0 + g * NU + b
                    if b + 2 < NB or not last:
                        normalise(b % 2, n + 2, n + 1)
                    ahead, k = piece_at(b)
                    if not (ahead and last):
                        half, head = PIECES[k]
                        pool.wait_ge(s_ready, ONE + CROSS0 + (g + ahead - 1) * NU + half * 4 + 4)
                        rotary_sum(g * 8 + LEAD + b, half, head, b % 2)

            with pool.Fori(0, NG // 2 - 1) as g2:
                for i in range(2):
                    group(g2 * 2 + i, False)
            group(NG - 2, False)
            group(NG - 1, True)

        @block.scalar
        def _(act):
            for started in (xnT_ready, cxT_ready, v_ready, vx_ready, qT_ready, kxT_ready, exp_done, pT_ready,
                            at_ready, oT_ready):
                act.sem_inc(started, ONE)
            act.wait_ge(eps_set, 1)

            def spread_of(n):
                act.wait_ge(mv_done, n * NB + NB)
                nc.scalar.activation(spread[:], mean_var[:, :, 1], ACT.Sqrt, bias=eps[:, 0:1])\
                    .then_inc(spread_done, 1)

            def exponentials(i, n, used):
                act.wait_ge(masked, ONE + n + 1)
                act.wait_ge(prob_ready, ONE + used)
                for h in range(UH):
                    last = nc.scalar.activation(exps[:, i, h, :], neg_scores[:, i, h, :], ACT.Exp,
                                                bias=neg_max[:, i, h:h + 1], scale=-1.0,
                                                accum_out=sums[:, i, h:h + 1])
                last.then_inc(exp_done, 1)

            def take_probsT(i, n, used, ps):
                act.wait_ge(pT_ps, ONE + n + 1)
                act.wait_ge(av_done, ONE + used)
                nc.scalar.copy(probsT[:, i], ps[:].rearrange("p (h q) -> p h q", h=UH)).then_inc(pT_ready, 1)

            spread_of(0)
            act.wait_ge(vz_zero, 1)
            with act.Fori(0, NB) as b:
                act.wait_ge(cxT_ps, ONE + b + 1)
                act.wait_ge(vx_ps, ONE + 2 * b)
                nc.scalar.copy(cxT[:], bank[6][:].rearrange("p (c t) -> p c t", c=EC)).then_inc(cxT_ready, 1)
                act.wait_ge(xnT_ps, ONE + b + 1)
                act.wait_ge(kv_ps, ONE + b)
                nc.scalar.copy(xnT[:], bank[5][:].rearrange("p (c t) -> p c t", c=EC)).then_inc(xnT_ready, 1)
                act.wait_ge(kv_ps, ONE + b + 1)
                act.wait_ge(kab_done, ONE + b + 1)
                act.wait_ge(av_done, ONE + b * NU)
                nc.scalar.copy(vz[:].rearrange("p (g c) -> p g c", c=VZ)[:, :, 0:SD],
                               bank[7][:, P:2 * P].rearrange("p (g d) -> p g d", d=SD)).then_inc(v_ready, 1)
                act.wait_ge(kv_stored, STORE_ONE + 32 * b)
                for i in range(2):
                    act.wait_ge(vx_ps, ONE + 2 * b + i + 1)
                    nc.scalar.copy(vx[:, i * 512:(i + 1) * 512], bank[2 + i][:]).then_inc(vx_ready, 1)
                act.wait_ge(qT_ps, ONE + b + 1)
                act.wait_ge(s_ready, ONE + b * NU)
                nc.scalar.copy(qT[:], bank[7][:].rearrange("p (j t) -> p j t", j=GH)).then_inc(qT_ready, 1)
                for i in range(2):
                    act.wait_ge(kxT_ps, ONE + 2 * b + i + 1)
                    nc.scalar.copy(kxT[:, 4 * i:4 * i + 4, :], bank[5 + i][:].rearrange("p (g t) -> p g t", g=4))\
                        .then_inc(kxT_ready, 1)
                for u in range(2):
                    exponentials(u, b * NU + u, b * NU)
                for u in range(NU):
                    take_probsT(u % 2, b * NU + u, b * NU + max(u - 1, 0), bank[2 + u % 2])
                    if u + 2 < NU:
                        exponentials(u % 2, b * NU + u + 2, b * NU + u + 1)
                act.wait_ge(av_done, ONE + b * NU + NU)
                act.wait_ge(o_ps, ONE + b)
                nc.scalar.copy(atT[:], bank[4][:].rearrange("p (j t) -> p j t", j=GH)).then_inc(at_ready, 1)

            act.wait_ge(x1_ready, ONE + NB)
            act.wait_ge(kv_stored, STORE_ONE + 32 * NB)
            spread_of(1)
            for b in range(NB):
                act.wait_ge(tab_ps, b + 1)
                nc.scalar.copy(cosT[:, b * P:(b + 1) * P], bank[b % 2][:, 0:P])
                nc.scalar.copy(sinT[:, b * P:(b + 1) * P], bank[b % 2][:, P:2 * P]).then_inc(tab_ready, 1)
                act.wait_ge(xn2T_ps, b + 1)
                nc.scalar.copy(xn2T[:, :, b * P:(b + 1) * P], bank[2 + b % 2][:].rearrange("p (c t) -> p c t", c=EC))\
                    .then_inc(xn2T_ready, 1)
            for u in range(2):
                exponentials(u, CROSS0 + u, CROSS0 + u - 1)

            def group(g, last):
                for b in range(NB):
                    n = CROSS0 + g * NU + b
                    take_probsT(b % 2, n, n - 1, bank[4 + b % 2])
                    if b + 2 < NB or not last:
                        exponentials(b % 2, n + 2, n + 1)
                    act.wait_ge(av_done, ONE + n + 1)
                    act.wait_ge(y_done, ONE + g * NU + b)
                    nc.scalar.copy(oT[:], bank[6][:].rearrange("p (h q) -> p h q", h=GH)).then_inc(oT_ready, 1)

            with act.Fori(0, NG // 2 - 1) as g2:
                for i in range(2):
                    group(g2 * 2 + i, False)
            group(NG - 2, False)
            group(NG - 1, True)
            spread_of(2)
            act.wait_ge(rwT_ps, 1)
            nc.scalar.copy(rwT[:], bank[7][:, 0:EC * NE].rearrange("p (c n) -> p c n", c=EC)).then_inc(rwT_ready, 1)
            for b in range(NB):
                act.wait_ge(xn3T_ps, b + 1)
                nc.scalar.copy(xn3T[:, :, b * P:(b + 1) * P], bank[b % 4][:].rearrange("p (c t) -> p c t", c=EC))\
                    .then_inc(xn3T_ready, 1)
            act.wait_ge(ffn_step, 3)
            nc.scalar.activation(lex[:], lsh[:], ACT.Exp).then_inc(lex_done, 1)
            for h in range(2):
                act.wait_ge(wdT_ps, h + 1)
                nc.scalar.copy(wdT[:, h * 512:(h + 1) * 512], bank[4 + h][0:NE, :]).then_inc(wdT_ready, 1)

        @block.vector
        def _(dve):
            for started in (xn_ready, qab_done, kab_done, kr_ready, kxab_done, kTz_ready, masked, rsum_ready,
                            x1_ready, rope_ab, acc_done):
                dve.sem_inc(started, ONE)
            nc.vector.memset(eps[:], EPS).then_inc(eps_set, 1)

            def statistics(b, n):
                nc.vector.bn_stats(stats[:], row(X, b)).then_inc(stats_done, 1)
                dve.wait_ge(stats_done, n + 1)
                dve.sem_inc(dve_passed)
                nc.vector.bn_aggr(one_row[:], stats[:]).then_inc(aggr_done, 1)
                dve.wait_ge(aggr_done, n + 1)
                dve.sem_inc(dve_passed)
                nc.vector.tensor_copy(row(mean_var, b), one_row[:]).then_inc(mv_done, 1)
                dve.wait_ge(mv_done, n + 1)

            def invert_spread(n):
                dve.wait_ge(spread_done, n + 1)
                nc.vector.reciprocal(rstd[:], spread[:]).then_inc(rstd_done, 1)
                dve.wait_ge(rstd_done, n + 1)

            def normed(to, b):
                return nc.vector.tensor_scalar(to, row(X, b), row(mean_var, b)[:, 0:1], rstd[:, bass.ds(b, 1)],
                                               ALU.subtract, ALU.mult)

            dve.wait_ge(pos_in, 16)
            nc.vector.tensor_scalar(posf[:], posi[:], 0.0, float(MAXPOS), ALU.is_lt, ALU.mult).then_inc(pos_a, 1)
            dve.wait_ge(pos_a, 1)
            nc.vector.tensor_tensor(posn[:], posi[:], posf[:], ALU.add).then_inc(pos_b, 1)
            dve.wait_ge(pos_b, 1)
            nc.vector.tensor_scalar(posu[:], posn[:], 0.0, float(MAXPOS - 1), ALU.max, ALU.min).then_inc(pos_ready, 1)
            for b in range(NB):
                dve.wait_ge(x_in[b], 16)
                statistics(b, b)
            invert_spread(0)
            dve.wait_ge(small_in, 48)
            dve.wait_ge(gathered, 16 * NB)

            def mask_scores(i, n, used, ps, added, scale):
                dve.wait_ge(s_ready, ONE + n + 1)
                dve.wait_ge(exp_done, ONE + used)
                dve.sem_inc(dve_passed)
                for h in range(UH):
                    last = nc.vector.tensor_tensor_reduce(
                        out=neg_scores[:, i, h, :], in0=ps[:, h * P:(h + 1) * P], in1=added, scale=-scale,
                        scalar=BIG, op0=ALU.add, op1=ALU.min, accum_out=neg_max[:, i, h:h + 1])
                last.then_inc(masked, 1)

            def invert_sums(i, n):
                dve.wait_ge(exp_done, ONE + n + 1)
                nc.vector.reciprocal(rsums[:, i], sums[:, i]).then_inc(rsum_ready, 1)

            def rotate(to_a, to_b, src, heads, width, cos, sin_low, sin_high):
                half = width // 2
                v, a, b_ = (t.rearrange("p (h d) -> p h d", d=width) for t in (src, to_a, to_b))
                nc.vector.tensor_tensor(a, v, cos.unsqueeze(1).to_broadcast([P, heads, width]), ALU.mult)
                nc.vector.tensor_tensor(b_[:, :, 0:half], v[:, :, half:width],
                                        sin_low.unsqueeze(1).to_broadcast([P, heads, half]), ALU.mult)
                return nc.vector.tensor_tensor(b_[:, :, half:width], v[:, :, 0:half],
                                               sin_high.unsqueeze(1).to_broadcast([P, heads, half]), ALU.mult)

            with dve.Fori(0, NB) as b:
                dve.wait_ge(xnT_ps, ONE + b)
                normed(xn[:], b).then_inc(xn_ready, 1)
                dve.wait_ge(q_ps, ONE + b + 1)
                dve.wait_ge(qr_ready, ONE + b)
                rotate(qa[:], qb[:], bank[5][:], E // SD, SD, rope_s[:, 0:SD], rope_s[:, SD:SD + 8],
                       rope_s[:, SD + 8:2 * SD]).then_inc(qab_done, 1)
                dve.wait_ge(kv_ps, ONE + b + 1)
                dve.wait_ge(kr_ready, ONE + b)
                rotate(ka[:], kb[:], bank[7][:, 0:P], NG, SD, rope_s[:, 0:SD], rope_s[:, SD:SD + 8],
                       rope_s[:, SD + 8:2 * SD]).then_inc(kab_done, 1)
                dve.wait_ge(kab_done, ONE + b + 1)
                dve.wait_ge(kT_ps, ONE + b)
                nc.vector.tensor_tensor(kr[:], ka[:], kb[:], ALU.add).then_inc(kr_ready, 1)
                tab = row(rope_x, b)
                dve.wait_ge(kxr_ready, ONE + 2 * b)
                for i in range(2):
                    dve.wait_ge(kx_ps, ONE + 2 * b + i + 1)
                    rotate(kxa[:, i], kxb[:, i], bank[i][:], 4, XD, tab[:, 0:128], tab[:, 192:256], tab[:, 128:192])\
                        .then_inc(kxab_done, 1)
                dve.wait_ge(kT_ps, ONE + b + 1)
                dve.wait_ge(s_ready, ONE + b * NU)
                nc.vector.tensor_tensor(kTz[:], bank[4][:, 0:P].unsqueeze(1).to_broadcast([P, NG, P]),
                                        rows[:].unsqueeze(2).to_broadcast([P, NG, P]), ALU.mult)\
                    .then_inc(kTz_ready, 1)
                for u in range(NU):
                    mask_scores(u % 2, b * NU + u, b * NU + max(u - 1, 0), bank[u % 2], causal[:], SELF_SCALE)
                    invert_sums(u % 2, b * NU + u)
                dve.wait_ge(o_ps, ONE + b + 1)
                nc.vector.tensor_tensor(row(X, b), bank[6][:], row(X, b), ALU.add).then_inc(x1_ready, 1)
                dve.wait_ge(x1_ready, ONE + b + 1)
                dve.sem_inc(dve_passed)
                statistics(b, b + NB)

            dve.wait_ge(kv_stored, STORE_ONE + 32 * NB)
            invert_spread(1)
            for b in range(NB):
                if b >= 2:
                    dve.wait_ge(xn2T_ps, b - 1)
                normed(xn2[:, b % 2], b).then_inc(xn2_ready, 1)
            dve.wait_ge(mask_in, 16)
            nc.vector.tensor_scalar(bias[:], maski[:], 0.0, NEG, ALU.is_equal, ALU.mult).then_inc(bias_ready, 1)
            dve.wait_ge(bias_ready, 1)
            dve.wait_ge(tab_ready, NB)

            def rotate_piece(m, half, i):
                dve.wait_ge(qp_done, ONE + m + 1)
                dve.wait_ge(q_ready, ONE + m - 1 if not isinstance(m, int) else ONE + max(m - 1, 0))
                t = slice(half * HALF_TOK, (half + 1) * HALF_TOK)
                lo, hi = slice(0, XD // 2), slice(XD // 2, XD)
                nc.vector.tensor_tensor(ra[:, i], bank[i][:], cosT[:, t], ALU.mult)
                nc.vector.tensor_tensor(rb[lo, i], bank[i][hi, :], sinT[hi, t], ALU.mult)
                nc.vector.tensor_tensor(rb[hi, i], bank[i][lo, :], sinT[lo, t], ALU.mult).then_inc(rope_ab, 1)

            for m in range(LEAD):
                rotate_piece(m, PIECES[m][0], m % 2)
            for u in range(2):
                mask_scores(u, CROSS0 + u, CROSS0 + u - 1, bank[2 + u], bias[:, u, :], CROSS_SCALE)
                invert_sums(u, CROSS0 + u)

            def group(g, last):
                for b in range(NB):
                    n = CROSS0 + g * NU + b
                    if b + 2 < NB or not last:
                        mask_scores(b % 2, n + 2, n + 1, bank[2 + b % 2], bias[:, (b + 2) % NB, :], CROSS_SCALE)
                        invert_sums(b % 2, n + 2)
                    ahead, k = piece_at(b)
                    if not (ahead and last):
                        rotate_piece(g * 8 + LEAD + b, PIECES[k][0], b % 2)
                    dve.wait_ge(y_done, ONE + g * NU + b + 1)
                    dve.wait_ge(acc_done, ONE + g * NU + b)
                    nc.vector.tensor_tensor(X[:, b, :], bank[7][:], X[:, b, :], ALU.add).then_inc(acc_done, 1)
                    if last:
                        dve.wait_ge(acc_done, ONE + g * NU + b + 1)
                        statistics(b, 2 * NB + b)

            with dve.Fori(0, NG // 2 - 1) as g2:
                for i in range(2):
                    group(g2 * 2 + i, False)
            group(NG - 2, False)
            group(NG - 1, True)

            invert_spread(2)
            for b in range(NB):
                normed(xn3[:, b, :], b).then_inc(xn3_ready, 1)
            dve.wait_ge(ffn_in, 48)
            dve.wait_ge(lg_ps, 1)

            steps = [0]

            def step(ins):
                steps[0] += 1
                ins.then_inc(ffn_step, 1)
                dve.wait_ge(ffn_step, steps[0])

            wide = [P, NB, NE]
            step(nc.vector.tensor_tensor(lg[:], bank[6][:].rearrange("p (b n) -> p b n", b=NB),
                                         rb_row[:].unsqueeze(1).to_broadcast(wide), ALU.add))
            step(nc.vector.tensor_reduce(lmax[:], lg[:], AX.X, ALU.max))
            step(nc.vector.tensor_tensor(lsh[:], lg[:], lmax[:].unsqueeze(2).to_broadcast(wide), ALU.subtract))
            dve.wait_ge(lex_done, 1)
            step(nc.vector.tensor_reduce(lsum[:], lex[:], AX.X, ALU.add))
            step(nc.vector.reciprocal(lrs[:], lsum[:]))
            step(nc.vector.tensor_tensor(lsc[:], lex[:], lrs[:].unsqueeze(2).to_broadcast(wide), ALU.mult))
            for b in range(NB):
                last = nc.vector.max(top[:, b, :], lsc[:, b, :])
            step(last)
            for b in range(NB):
                last = nc.vector.match_replace(out=cut[:, b, :], in_to_replace=top[:, b, :],
                                               in_values=lsc[:, b, :], imm_value=-1.0)
            step(last)
            step(nc.vector.scalar_tensor_tensor(out=wd[:], in0=cut[:], scalar=0.0, in1=lsc[:], op0=ALU.is_lt,
                                                op1=ALU.mult))
            step(nc.vector.tensor_reduce(wsum[:], wd[:], AX.X, ALU.add))
            for b in range(NB):
                last = nc.vector.scalar_tensor_tensor(out=X[:, b, :], in0=xn3[:, b, :], scalar=wsum[:, b:b + 1],
                                                      in1=X[:, b, :], op0=ALU.mult, op1=ALU.add)
            step(last)
            for b in range(NB):
                dve.wait_ge(mix_ps, b + 1)
                nc.vector.tensor_tensor(xn3[:, b, :], bank[b % 4][:], X[:, b, :], ALU.add).then_inc(fin_ready, 1)

        @block.tensor
        def _(pe):
            for started in (xnT_ps, cxT_ps, q_ps, kv_ps, kx_ps, vx_ps, qT_ps, kT_ps, kxT_ps, o_ps, s_ready, pT_ps,
                            av_done, qp_done, y_done):
                pe.sem_inc(started, ONE)
            pe.wait_ge(ident_in, 16)
            pe.wait_ge(wqkv_in, 48)
            pe.wait_ge(wkv2_in, 32)
            pe.wait_ge(wo1_in, 16 * NG)

            def transpose_chunks(ps, src, n=4):
                for c in range(n):
                    last = nc.tensor.transpose(ps[:, c * P:(c + 1) * P], src[:, c * P:(c + 1) * P], ident[:])
                return last

            def product(ps, lhsT, rhs):
                for c in range(EC):
                    last = nc.tensor.matmul(ps, lhsT(c), rhs(c), start=(c == 0), stop=(c == EC - 1))
                return last

            def transpose_probs(i, n, ps):
                pe.wait_ge(prob_ready, ONE + n + 1)
                for h in range(UH):
                    last = nc.tensor.transpose(ps[:, h * P:(h + 1) * P], probs[:, i, h, :], ident[:])
                last.then_inc(pT_ps, 1)

            with pe.Fori(0, NB) as b:
                pe.wait_ge(ctx_in_, 16 * b + 16)
                pe.wait_ge(x1_ready, ONE + b)
                transpose_chunks(bank[6], cx).then_inc(cxT_ps, 1)
                pe.wait_ge(xn_ready, ONE + b + 1)
                pe.wait_ge(kxT_ready, ONE + 2 * b)
                transpose_chunks(bank[5], xn).then_inc(xnT_ps, 1)
                pe.wait_ge(xnT_ready, ONE + b + 1)
                product(bank[5][:], lambda c: xnT[:, c, :], lambda c: wq1[:, c, :]).then_inc(q_ps, 1)
                pe.wait_ge(qT_ready, ONE + b)
                product(bank[7][:, 0:2 * P], lambda c: xnT[:, c, :], lambda c: wkv1[:, c, :]).then_inc(kv_ps, 1)
                pe.wait_ge(cxT_ready, ONE + b + 1)
                pe.wait_ge(masked, ONE + b * NU)
                for i in range(2):
                    product(bank[i][:], lambda c: cxT[:, c, :], lambda c: wk2[:, c, i * 512:(i + 1) * 512])\
                        .then_inc(kx_ps, 1)
                pe.wait_ge(pT_ready, ONE + b * NU)
                for i in range(2):
                    product(bank[2 + i][:], lambda c: cxT[:, c, :], lambda c: wv2[:, c, i * 512:(i + 1) * 512])\
                        .then_inc(vx_ps, 1)
                pe.wait_ge(qr_ready, ONE + b + 1)
                pe.wait_ge(kab_done, ONE + b + 1)
                pe.wait_ge(v_ready, ONE + b + 1)
                transpose_chunks(bank[7], qr).then_inc(qT_ps, 1)
                pe.wait_ge(kr_ready, ONE + b + 1)
                pe.wait_ge(at_ready, ONE + b)
                nc.tensor.transpose(bank[4][:, 0:P], kr[:], ident[:]).then_inc(kT_ps, 1)
                for i in range(2):
                    pe.wait_ge(kxr_ready, ONE + 2 * b + i + 1)
                    transpose_chunks(bank[5 + i], kxr[:, i]).then_inc(kxT_ps, 1)

                def scores(u):
                    nc.tensor.matmul(bank[u % 2][:], qT[:, u // 2, :], kTz[:, 4 * (u % 2):4 * (u % 2) + 4, :],
                                     start=True, stop=True).then_inc(s_ready, 1)

                pe.wait_ge(qT_ready, ONE + b + 1)
                pe.wait_ge(kTz_ready, ONE + b + 1)
                for u in range(2):
                    pe.wait_ge(kxab_done, ONE + 2 * b + u + 1)
                    scores(u)
                for u in range(NU):
                    n = b * NU + u
                    if u < 2:
                        pe.wait_ge(vx_ready, ONE + 2 * b + u + 1)
                    else:
                        pe.wait_ge(pT_ready, ONE + n - 1)
                    transpose_probs(u % 2, n, bank[2 + u % 2])
                    if u + 2 < NU:
                        pe.wait_ge(masked, ONE + n + 1)
                        scores(u + 2)
                    pe.wait_ge(pT_ready, ONE + n + 1)
                    j, half = u // 2, u % 2
                    for i in range(UH):
                        g = UH * half + i
                        last = nc.tensor.matmul(bank[4][:, j * P:(j + 1) * P], vz[:, g * P:(g + 1) * P],
                                                probsT[:, u % 2, i, :], start=(g == 0), stop=(g == NG - 1))
                    last.then_inc(av_done, 1)
                pe.wait_ge(at_ready, ONE + b + 1)
                pe.wait_ge(kxT_ready, ONE + 2 * b + 2)
                for j in range(GH):
                    last = nc.tensor.matmul(bank[6][:], atT[:, j, :], wo1[:, j, :], start=(j == 0), stop=(j == GH - 1))
                last.then_inc(o_ps, 1)

            pe.wait_ge(gathered, 16 * NB)
            for b in range(NB):
                if b >= 2:
                    pe.wait_ge(tab_ready, b - 1)
                for i in range(2):
                    last = nc.tensor.transpose(bank[b % 2][:, i * P:(i + 1) * P], rope_x[:, b, i * P:(i + 1) * P],
                                               ident[:])
                last.then_inc(tab_ps, 1)
                if b >= 2:
                    pe.wait_ge(xn2T_ready, b - 1)
                pe.wait_ge(xn2_ready, b + 1)
                transpose_chunks(bank[2 + b % 2], xn2[:, b % 2]).then_inc(xn2T_ps, 1)
            pe.wait_ge(tab_ready, NB)
            pe.wait_ge(xn2T_ready, NB)

            def make_piece(m, g, half, head, i):
                pe.wait_ge(wq_in[head], 16 * (g + 1))
                pe.wait_ge(rope_ab, ONE + m - 1 if not isinstance(m, int) else ONE + max(m - 1, 0))
                t = slice(half * HALF_TOK, (half + 1) * HALF_TOK)
                product(bank[i][:], lambda c: wq_g[:, head, c, :], lambda c: xn2T[:, c, t]).then_inc(qp_done, 1)

            def cross_scores(n, g, b, i):
                pe.wait_ge(masked, ONE + n - 1)
                pe.wait_ge(kv_in, 32 * (g + 1))
                pe.wait_ge(q_ready, ONE + g * 8 + (b // 4) * 4 + 4)
                for h in range(GH):
                    last = nc.tensor.matmul(bank[2 + b % 2][:, h * P:(h + 1) * P], Q[:, h, b * P:(b + 1) * P],
                                            k_g[:, i, b * P:(b + 1) * P], start=True, stop=True)
                last.then_inc(s_ready, 1)

            for m in range(LEAD):
                make_piece(m, 0, *PIECES[m], m % 2)
            for b in range(2):
                cross_scores(CROSS0 + b, 0, b, 0)

            def group(g, i, last_group):
                for b in range(NB):
                    n = CROSS0 + g * NU + b
                    pe.wait_ge(pT_ready, ONE + n - 1)
                    transpose_probs(b % 2, n, bank[4 + b % 2])
                    if b + 2 < NB:
                        cross_scores(n + 2, g, b + 2, i)
                    elif not last_group:
                        cross_scores(n + 2, g + 1, b + 2 - NB, 1 - i)
                    pe.wait_ge(pT_ready, ONE + n + 1)
                    pe.wait_ge(oT_ready, ONE + g * NU + b)
                    nc.tensor.matmul(bank[6][:], v_g[:, i, b, :], probsT[:, b % 2], start=True, stop=True)\
                        .then_inc(av_done, 1)
                    ahead, k = piece_at(b)
                    if not (ahead and last_group):
                        half, head = PIECES[k]
                        make_piece(g * 8 + LEAD + b, g + ahead, half, head, b % 2)
                    pe.wait_ge(wo_in, 16 * (g + 1))
                    pe.wait_ge(oT_ready, ONE + g * NU + b + 1)
                    pe.wait_ge(acc_done, ONE + g * NU + b)
                    for h in range(GH):
                        last = nc.tensor.matmul(bank[7][:], oT[:, h, :], wo_g[:, i, h, :], start=(h == 0),
                                                stop=(h == GH - 1))
                    last.then_inc(y_done, 1)

            with pe.Fori(0, NG // 2 - 1) as g2:
                for i in range(2):
                    group(g2 * 2 + i, i, False)
            group(NG - 2, 0, False)
            group(NG - 1, 1, True)

            pe.wait_ge(ffn_in, 48)
            pe.wait_ge(acc_done, ONE + NG * NU)
            for c in range(EC):
                last = nc.tensor.transpose(bank[7][:, c * NE:(c + 1) * NE], rw[:, c * P:(c + 1) * P],
                                           ident[0:NE, 0:NE])
            last.then_inc(rwT_ps, 1)
            pe.wait_ge(oT_ready, ONE + NG * NU)
            for b in range(NB):
                if b >= 4:
                    pe.wait_ge(xn3T_ready, b - 3)
                pe.wait_ge(xn3_ready, b + 1)
                transpose_chunks(bank[b % 4], xn3[:, b, :]).then_inc(xn3T_ps, 1)
            pe.wait_ge(rwT_ready, 1)
            for b in range(NB):
                pe.wait_ge(xn3T_ready, b + 1)
                last = product(bank[6][:, b * NE:(b + 1) * NE], lambda c: xn3T[:, c, b * P:(b + 1) * P],
                               lambda c: rwT[:, c, :])
            last.then_inc(lg_ps, 1)
            pe.wait_ge(ffn_step, 9)
            for h in range(2):
                for k in range(4):
                    last = nc.tensor.transpose(bank[4 + h][0:NE, k * P:(k + 1) * P], wd[:, 4 * h + k, :], ident[:])
                last.then_inc(wdT_ps, 1)
            for b in range(NB):
                pe.wait_ge(wdT_ready, b // 4 + 1)
                if b >= 4:
                    pe.wait_ge(fin_ready, b - 3)
                nc.tensor.matmul(bank[b % 4][:], wdT[:, b * P:(b + 1) * P], eb[:], start=True, stop=True)\
                    .then_inc(mix_ps, 1)


def constants():
    import numpy as np

    f = np.float32
    steps = np.arange(P, dtype=f)
    inv = (f(1) / f(500000.0) ** (np.arange(0, SD, 2, dtype=f) / f(SD))).astype(f)
    angle = (steps[:, None] * inv[None, :]).astype(f)
    c, s = np.cos(angle), np.sin(angle)
    rope_self = np.concatenate([c, c, -s, s], 1).astype(f)
    inv = (f(1) / f(10000.0) ** (np.arange(0, XD, 2, dtype=f) / f(XD))).astype(f)
    angle = (np.arange(MAXPOS, dtype=f)[:, None] * inv[None, :]).astype(f)
    c, s = np.cos(angle), np.sin(angle)
    rope_cross = np.concatenate([c, c, s, -s], 1).astype(f)
    causal = np.where(np.triu(np.ones((P, P), bool), 1), f(NEG), f(0)).astype(f)
    rows = (np.arange(P)[:, None] // SD == np.arange(NG)[None, :]).astype(f)
    return {"c_ident": np.eye(P, dtype=f), "c_causal": causal, "c_rope_self": rope_self,
            "c_rope_cross": rope_cross, "c_rows": rows}


_INS = ["x", "ctx_4096", "pos_BxS2", "mask_BxSxS2_ik0", "L0_attn_Wq", "L0_attn_Wk", "L0_attn_Wv", "L0_attn_Wo",
        "L0_xattn_Wq", "L0_xattn_Wk", "L0_xattn_Wv", "L0_xattn_Wo", "L0_ffn_router_weight", "L0_ffn_router_bias",
        "L0_ffn_expert_bias"]


def kernel(**inputs):
    import numpy as _np
    import concourse.bacc as _bacc
    from concourse import mybir as _mybir
    from concourse.bass_utils import run_bass_kernel_spmd as _run

    nc = _bacc.Bacc("TRN2", target_bir_lowering=False, num_devices=1)
    arrays, args = {}, []
    for name, a in [(n, inputs[n]) for n in _INS] + list(constants().items()):
        a = _np.ascontiguousarray(_np.transpose(a) if name == "pos_BxS2" else a)
        arrays[f"in_{name}"] = a
        args.append(nc.dram_tensor(f"in_{name}", a.shape, _mybir.dt.from_np(a.dtype), kind="ExternalInput").ap())
    args.append(nc.dram_tensor("out_0", (NB, P, E), F32, kind="ExternalOutput").ap())
    decoder(nc, *args)
    r = _run(nc, [arrays], core_ids=[0])
    return r.results[0]["out_0"]
```

```python
from contextlib import ExitStack
import math

import concourse.bass as bass
from concourse import mybir

F32 = mybir.dt.float32
F32R = mybir.dt.float32r
I32 = mybir.dt.int32
U32 = mybir.dt.uint32
ALU = mybir.AluOpType
ACT = mybir.ActivationFunctionType
AX = mybir.AxisListType

P = 128
NB = 8
E = 512
EC = E // P
NU = 8
UH = 4
NG = 8
GH = 4
SD = 16
XD = 128
MAXPOS = 512
SELF_SCALE = 1.0 / math.sqrt(SD)
CROSS_SCALE = 1.0 / math.sqrt(XD)
NEG = -float(2 ** 100)
BIG = 3.0e38
EPS = 1e-5
NE = 64
TOP = 8
RING = 4
VZ = 9 * SD
HALF_TOK = 4 * P


def decoder(nc, x, ctx, pos, mask, wq_s, wk_s, wv_s, wo_s, wq_x, wk_x, wv_x, wo_x,
            router_w, router_b, expert_b, c_ident, c_causal, c_rope_self, c_rope_cross, c_rows, out):
    k_dram = nc.dram_tensor("k_cross", (NG, XD, NB * P), F32, kind="Internal").ap()
    v_dram = nc.dram_tensor("v_cross", (NB, P, NG * XD), F32, kind="Internal").ap()

    with ExitStack() as whole:
        def sem(name):
            return whole.enter_context(nc.semaphore(name))

        def keep(name, shape, dt=F32):
            return whole.enter_context(nc.sbuf_tensor(name, shape, dt))

        bank = [whole.enter_context(nc.psum_tensor(f"bank{i}", [P, 512], F32)) for i in range(8)]

        ident = keep("ident", [P, P])
        X = keep("X", [P, NB, E])
        rope_x = keep("rope_x", [P, NB, 4 * 64])
        mean_var = keep("mean_var", [P, NB, 2])
        stats = keep("stats", [P, NB, 6])
        one_row = keep("one_row", [P, 2])
        spread = keep("spread", [P, NB])
        rstd = keep("rstd", [P, NB])
        eps = keep("eps", [P, 1])
        unused = keep("unused", [P, 1])
        neg_scores = keep("neg_scores", [P, 2, UH, P])
        neg_max = keep("neg_max", [P, 2, UH])
        exps = keep("exps", [P, 2, UH, P])
        sums = keep("sums", [P, 2, UH])
        rsums = keep("rsums", [P, 2, UH])
        probs = keep("probs", [P, 2, UH, P])
        probsT = keep("probsT", [P, 2, UH, P])
        ring = keep("ring", [P, RING, 512])

        first = ExitStack()

        def one(name, shape, dt=F32):
            return first.enter_context(nc.sbuf_tensor(name, shape, dt))

        causal = one("causal", [P, P])
        rope_s = one("rope_s", [P, 2 * SD])
        rows = one("rows", [P, NG])
        wq1_h, wq1_l = one("wq1_h", [P, EC, E], F32R), one("wq1_l", [P, EC, E], F32R)
        wkv1_h, wkv1_l = one("wkv1_h", [P, EC, 2 * P], F32R), one("wkv1_l", [P, EC, 2 * P], F32R)
        wk2_h, wk2_l = one("wk2_h", [P, EC, NG * XD], F32R), one("wk2_l", [P, EC, NG * XD], F32R)
        wv2_h, wv2_l = one("wv2_h", [P, EC, NG * XD], F32R), one("wv2_l", [P, EC, NG * XD], F32R)
        wo1 = one("wo1", [P, GH, E])
        posi = one("posi", [P, NB], I32)
        posf = one("posf", [P, NB])
        posn = one("posn", [P, NB])
        posu = one("posu", [P, NB], U32)
        xn = one("xn", [P, E])
        xnT_h, xnT_l = one("xnT_h", [P, EC, P], F32R), one("xnT_l", [P, EC, P], F32R)
        cx = one("cx", [P, E])
        cxT_h, cxT_l = one("cxT_h", [P, EC, P], F32R), one("cxT_l", [P, EC, P], F32R)
        qa = one("qa", [P, E])
        qb = one("qb", [P, E])
        qr = one("qr", [P, E])
        ka = one("ka", [P, P])
        kb = one("kb", [P, P])
        kr = one("kr", [P, P])
        vs = one("vs", [P, P])
        kxa = one("kxa", [P, E])
        kxb = one("kxb", [P, E])
        kxr = one("kxr", [P, 2, E])
        kxT = one("kxT", [P, NG, P])
        vx = one("vx", [P, NG * XD])
        qT_h, qT_l = one("qT_h", [P, GH, P], F32R), one("qT_l", [P, GH, P], F32R)
        kT_h, kT_l = one("kT_h", [P, P], F32R), one("kT_l", [P, P])
        kTz_h, kTz_l = one("kTz_h", [P, NG, P], F32R), one("kTz_l", [P, NG, P], F32R)
        vz = one("vz", [P, NG * VZ])
        atT = one("atT", [P, GH, P])
        first.close()

        second = ExitStack()

        def two(name, shape, dt=F32):
            return second.enter_context(nc.sbuf_tensor(name, shape, dt))

        k_g = two("k_g", [P, 2, NB * P])
        v_g = two("v_g", [P, 2, NB, XD])
        wq_h, wq_l = two("wq_h", [P, GH, EC, XD], F32R), two("wq_l", [P, GH, EC, XD], F32R)
        wo_h, wo_l = two("wo_h", [P, 2, GH, E], F32R), two("wo_l", [P, 2, GH, E], F32R)
        Q = two("Q", [P, GH, NB * P])
        cosT = two("cosT", [P, NB * P])
        sinT = two("sinT", [P, NB * P])
        ra = two("ra", [P, 2, HALF_TOK])
        rb = two("rb", [P, 2, HALF_TOK])
        xn2 = two("xn2", [P, 2, E])
        xn2T_h, xn2T_l = two("xn2T_h", [P, EC, NB * P], F32R), two("xn2T_l", [P, EC, NB * P], F32R)
        maski = two("maski", [P, NB, P], I32)
        bias = two("bias", [P, NB, P])
        oT_h, oT_l = two("oT_h", [P, GH, P], F32R), two("oT_l", [P, GH, P], F32R)
        second.close()

        third = ExitStack()

        def three(name, shape, dt=F32):
            return third.enter_context(nc.sbuf_tensor(name, shape, dt))

        xn3 = three("xn3", [P, NB, E])
        xn3T = three("xn3T", [P, EC, NB * P])
        rw = three("rw", [NE, E])
        rwT = three("rwT", [P, EC, NE])
        rb_row = three("rb_row", [P, NE])
        eb = three("eb", [NE, E])
        lg = three("lg", [P, NB, NE])
        lmax = three("lmax", [P, NB])
        lsum = three("lsum", [P, NB])
        lrs = three("lrs", [P, NB])
        lsh = three("lsh", [P, NB, NE])
        lex = three("lex", [P, NB, NE])
        lsc = three("lsc", [P, NB, NE])
        top = three("top", [P, NB, TOP])
        cut = three("cut", [P, NB, NE])
        wd = three("wd", [P, NB, NE])
        wsum = three("wsum", [P, NB])
        wdT = three("wdT", [NE, NB * P])
        third.close()

        x_in = [sem(f"x_in{b}") for b in range(NB)]
        weight_in = [sem(f"weight_in{k}") for k in range(11)]
        ring_in = [sem(f"ring_in{i}") for i in range(RING)]
        ident_in, small_in, pos_in = sem("ident_in"), sem("small_in"), sem("pos_in")
        wo1_in, ctx_in_, gathered, kv_in = sem("wo1_in"), sem("ctx_in"), sem("gathered"), sem("kv_in")
        weight_h, weight_l, v_weight_l = sem("weight_h"), sem("weight_l"), sem("v_weight_l")
        ring_h, ring_l = sem("ring_h"), sem("ring_l")
        mask_in, ffn_in, stored, kv_stored = sem("mask_in"), sem("ffn_in"), sem("stored"), sem("kv_stored")
        eps_set, stats_done, aggr_done, mv_done = sem("eps_set"), sem("stats_done"), sem("aggr_done"), sem("mv_done")
        spread_done, rstd_done = sem("spread_done"), sem("rstd_done")
        pos_a, pos_b, pos_ready = sem("pos_a"), sem("pos_b"), sem("pos_ready")
        vz_zero = sem("vz_zero")
        xn_ready, xnT_ps, xnT_hs, xnT_ls = sem("xn_ready"), sem("xnT_ps"), sem("xnT_hs"), sem("xnT_ls")
        cxT_ps, cxT_hs, cxT_ls = sem("cxT_ps"), sem("cxT_hs"), sem("cxT_ls")
        q_ps, kv_ps, kx_ps, vx_ps = sem("q_ps"), sem("kv_ps"), sem("kx_ps"), sem("vx_ps")
        qab_done, qr_ready, kab_done, kr_ready = sem("qab_done"), sem("qr_ready"), sem("kab_done"), sem("kr_ready")
        v_taken, v_ready, kxab_done = sem("v_taken"), sem("v_ready"), sem("kxab_done")
        kxr_ready, vx_ready = sem("kxr_ready"), sem("vx_ready")
        qT_ps, qT_hs, qT_ls, kT_ps, kT_hs, kT_ls = (sem(n) for n in ("qT_ps", "qT_hs", "qT_ls", "kT_ps", "kT_hs",
                                                                     "kT_ls"))
        kTz_hs, kTz_ls = sem("kTz_hs"), sem("kTz_ls")
        kxT_ps, kxT_ready = sem("kxT_ps"), sem("kxT_ready")
        at_ready, o_ps, x1_ready = sem("at_ready"), sem("o_ps"), sem("x1_ready")
        s_ready, masked, exp_done, rsum_ready = sem("s_ready"), sem("masked"), sem("exp_done"), sem("rsum_ready")
        prob_ready, pT_ps, pT_ready, av_done = sem("prob_ready"), sem("pT_ps"), sem("pT_ready"), sem("av_done")
        xn2_ready, xn2T_ps, xn2T_hs, xn2T_ls = sem("xn2_ready"), sem("xn2T_ps"), sem("xn2T_hs"), sem("xn2T_ls")
        tab_ps, tab_ready, bias_ready = sem("tab_ps"), sem("tab_ready"), sem("bias_ready")
        qp_done, rope_ab, q_ready = sem("qp_done"), sem("rope_ab"), sem("q_ready")
        oT_hs, oT_ls, y_done, acc_done = sem("oT_hs"), sem("oT_ls"), sem("y_done"), sem("acc_done")
        xn3_ready, xn3T_ps, xn3T_ready = sem("xn3_ready"), sem("xn3T_ps"), sem("xn3T_ready")
        rwT_ps, rwT_ready, lg_ps, ffn_step = sem("rwT_ps"), sem("rwT_ready"), sem("lg_ps"), sem("ffn_step")
        lex_done, wdT_ps, wdT_ready = sem("lex_done"), sem("wdT_ps"), sem("wdT_ready")
        mix_ps, fin_ready = sem("mix_ps"), sem("fin_ready")

        ONE, STORE_ONE = 1, 16
        sp_passed, dve_passed = sem("sp_passed"), sem("dve_passed")

        CROSS0 = NB * NU
        PIECES = [(half, head) for half in range(2) for head in range(GH)]
        LEAD = 7

        def piece_at(slot):
            n = slot + LEAD
            return (0, n) if n < 8 else (1, n - 8)

        def row(t, b):
            return t[:, bass.ds(b, 1), :].rearrange("p o n -> p (o n)")

        def as_read(t):
            return t.bitcast(F32)

        wq_d, wk_d, wv_d, wk2_d, wv2_d = (w.rearrange("(c p) n -> p c n", p=P) for w in (wq_s, wk_s, wv_s, wk_x, wv_x))
        weights1 = [(wq1_h[:, 2 * c:2 * c + 2, :], wq1_l[:, 2 * c:2 * c + 2, :], [wq_d[:, 2 * c:2 * c + 2, :]], 2)
                    for c in range(EC // 2)]
        weights1 += [(wkv1_h[:], wkv1_l[:], [wk_d, wv_d], EC)]
        weights1 += [(h[:, c:c + 1, :], l[:, c:c + 1, :], [d[:, c:c + 1, :]], 1)
                     for h, l, d in ((wk2_h, wk2_l, wk2_d), (wv2_h, wv2_l, wv2_d)) for c in range(EC)]
        SELF_W, KEY_W = range(0, 3), range(3, 7)
        VALUE_W = range(7, 11)
        places = [ring[:, 0:2, :], ring[:, 2:4, :], vx[:].rearrange("p (i n) -> p i n", i=2), kxT[:], kxr[:],
                  wo1[:, 0:2, :], wo1[:, 2:4, :]]

        def loaded(k):
            return places[k % len(places)].rearrange("p i n -> p (i n)").rearrange("p (c n) -> p c n",
                                                                                   c=weights1[k][3])

        block = whole.enter_context(nc.Block())

        @block.sync
        def _(sp):
            sp.sem_inc(kv_stored, STORE_ONE)
            sp.dma_start(ident[:], c_ident).then_inc(ident_in, 16)
            for b in range(NB):
                sp.dma_start(X[:, b, :], x[b]).then_inc(x_in[b], 16)
            sp.dma_start(cx[:], ctx[0]).then_inc(ctx_in_, 16)
            for k, (_, _, sources, blocks) in enumerate(weights1):
                if k >= len(places):
                    sp.wait_ge(weight_l, k - len(places) + 1)
                width = 2 * E // blocks // len(sources)
                for q, source in enumerate(sources):
                    sp.dma_start(loaded(k)[:, :, q * width:(q + 1) * width], source).then_inc(weight_in[k], 16)
            sp.wait_ge(weight_l, len(places))
            for g in range(NG):
                sp.dma_start(wo1[SD * g:SD * (g + 1), :, :],
                             wo_s[g * GH * SD:(g + 1) * GH * SD, :].rearrange("(j d) n -> d j n", d=SD))\
                    .then_inc(wo1_in, 16)

            sp.wait_ge(v_weight_l, 2)

            def cross_weights(g, u):
                if u < GH:
                    source = wq_x[:, bass.ds(g * (GH * XD) + u * XD, XD)].rearrange("(c p) n -> p c n", p=P)
                    to = ring[:, u % RING, :].rearrange("p (c n) -> p c n", c=EC)
                else:
                    source = wo_x[bass.ds(g * (GH * XD) + (u - GH) * XD, XD), :]
                    to = ring[:, u % RING, :]
                sp.dma_start(to, source).then_inc(ring_in[u % RING], 16)

            for u in range(RING):
                cross_weights(0, u)

            def row_stores(r, last):
                if not last:
                    sp.wait_ge(cxT_ps, ONE + r + 1)
                    sp.sem_inc(sp_passed)
                    sp.dma_start(cx[:], ctx[bass.ds(r + 1, 1)].rearrange("o p n -> p (o n)")).then_inc(ctx_in_, 16)
                sp.wait_ge(kxT_ready, ONE + 2 * r + 2)
                sp.sem_inc(sp_passed)
                sp.dma_start(k_dram[:, :, bass.ds(r * P, P)].rearrange("g d t -> d g t"), kxT[:])\
                    .then_inc(kv_stored, 16)
                sp.wait_ge(vx_ready, ONE + 2 * r + 2)
                sp.sem_inc(sp_passed)
                sp.dma_start(v_dram[bass.ds(r, 1)].rearrange("o p n -> p (o n)"), vx[:]).then_inc(kv_stored, 16)

            with sp.Fori(0, NB - 1) as r:
                row_stores(r, False)
            row_stores(NB - 1, True)
            sp.wait_ge(x1_ready, ONE + NB)
            sp.wait_ge(kv_stored, STORE_ONE + 32 * NB)
            sp.dma_start(maski[:], mask.rearrange("b q k -> q b k")).then_inc(mask_in, 16)
            sp.dma_start(k_g[:, 0, :], k_dram[0]).then_inc(kv_in, 16)
            sp.dma_start(v_g[:, 0, :, :], v_dram[:, :, 0:XD].rearrange("b k d -> k b d")).then_inc(kv_in, 16)
            for k in range(RING, 8 + RING):
                sp.wait_ge(ring_l, ONE + k - RING + 1)
                cross_weights(k // 8, k % 8)

            def next_group(g, i, last):
                sp.wait_ge(av_done, ONE + CROSS0 + g * NU)
                sp.sem_inc(sp_passed)
                sp.dma_start(k_g[:, 1 - i, :], k_dram[bass.ds(g + 1, 1)].rearrange("o d t -> d (o t)"))\
                    .then_inc(kv_in, 16)
                sp.dma_start(v_g[:, 1 - i, :, :], v_dram[:, :, bass.ds((g + 1) * XD, XD)]
                             .rearrange("b k d -> k b d")).then_inc(kv_in, 16)
                for k in range(RING, 8 if last else 8 + RING):
                    sp.wait_ge(ring_l, ONE + (g + 1) * 8 + k - RING + 1)
                    sp.sem_inc(sp_passed)
                    cross_weights(g + 1 + k // 8, k % 8)

            with sp.Fori(0, NG // 2 - 1) as g2:
                for i in range(2):
                    next_group(g2 * 2 + i, i, False)
            next_group(NG - 2, 0, True)
            sp.wait_ge(acc_done, ONE + NG * NU)
            sp.dma_start(rw[:], router_w).then_inc(ffn_in, 16)
            sp.dma_start(eb[:], expert_b).then_inc(ffn_in, 16)
            sp.dma_start(rb_row[:], router_b.rearrange("(o n) -> o n", o=1).to_broadcast([P, NE]))\
                .then_inc(ffn_in, 16)
            for b in range(NB):
                sp.wait_ge(fin_ready, b + 1)
                sp.dma_start(out[b], xn3[:, b, :]).then_inc(stored, 16)
            sp.wait_ge(stored, 16 * NB)

        @block.gpsimd
        def _(pool):
            for started in (qr_ready, kxr_ready, kTz_hs, prob_ready, q_ready, ring_l):
                pool.sem_inc(started, ONE)
            pool.dma_start(posi[:], pos).then_inc(pos_in, 16)
            pool.dma_start(rope_s[:], c_rope_self).then_inc(small_in, 16)
            pool.dma_start(rows[:], c_rows).then_inc(small_in, 16)
            pool.dma_start(causal[:], c_causal).then_inc(small_in, 16)
            nc.gpsimd.memset(vz[:], 0.0).then_inc(vz_zero, 1)
            pool.wait_ge(pos_ready, 1)
            for b in range(NB):
                pool.indirect_dma_start(out=rope_x[:, b, :], out_offset=None, in_=c_rope_cross,
                                        in_offset=bass.IndirectOffsetOnAxis(ap=posu[:, b:b + 1], axis=0))\
                    .then_inc(gathered, 16)

            def normalise(i, n, read):
                pool.wait_ge(rsum_ready, ONE + n + 1)
                pool.wait_ge(pT_ps, ONE + read)
                nc.gpsimd.tensor_tensor(probs[:, i], exps[:, i], rsums[:, i].unsqueeze(2).to_broadcast([P, UH, P]),
                                        ALU.mult).then_inc(prob_ready, 1)

            def query_sum(r):
                pool.wait_ge(qab_done, ONE + r + 1)
                pool.wait_ge(qT_ps, ONE + r)
                by_group = "p (g j d) -> p g j d"
                nc.gpsimd.tensor_tensor(qr[:].rearrange("p (j g d) -> p g j d", j=GH, g=NG),
                                        qa[:].rearrange(by_group, g=NG, j=GH), qb[:].rearrange(by_group, g=NG, j=GH),
                                        ALU.add).then_inc(qr_ready, 1)

            def spread_keys_high(r):
                pool.wait_ge(kT_hs, ONE + r + 1)
                pool.wait_ge(s_ready, ONE + r * NU)
                nc.gpsimd.tensor_tensor(kTz_h[:], as_read(kT_h[:]).unsqueeze(1).to_broadcast([P, NG, P]),
                                        rows[:].unsqueeze(2).to_broadcast([P, NG, P]), ALU.mult).then_inc(kTz_hs, 1)

            def cross_key_sum(r, i):
                pool.wait_ge(kxab_done, ONE + 2 * r + i + 1)
                pool.wait_ge(kxT_ps, ONE + 2 * r)
                nc.gpsimd.tensor_tensor(kxr[:, i], kxa[:], kxb[:], ALU.add).then_inc(kxr_ready, 1)

            def self_slot(r, u, last):
                n = r * NU + u
                if u == 6 and not last:
                    spread_keys_high(r + 1)
                if not last or u + 1 < NU:
                    normalise((u + 1) % 2, n + 1, n)
                if u < 2:
                    cross_key_sum(r, u)
                if u == 2 and not last:
                    query_sum(r + 1)

            def split_value_weights(ks):
                for k in ks:
                    pool.wait_ge(weight_h, k + 1)
                    high, part = weights1[k][0:2]
                    nc.gpsimd.tensor_tensor(part, loaded(k), as_read(high), ALU.subtract).then_inc(v_weight_l, 1)

            pool.wait_ge(small_in, 48)
            query_sum(0)
            spread_keys_high(0)
            split_value_weights(VALUE_W[0:2])
            normalise(0, 0, 0)
            self_slot(0, 0, False)
            split_value_weights(VALUE_W[2:4])
            with pool.Fori(0, NB - 1) as r:
                for u in range(1, NU):
                    self_slot(r, u, False)
                self_slot(r + 1, 0, False)
            for u in range(1, NU):
                self_slot(NB - 1, u, True)

            pool.wait_ge(x1_ready, ONE + NB)

            def split_low(g, i, u):
                piece = ring[:, u % RING, :]
                pool.wait_ge(ring_h, ONE + g * 8 + u + 1)
                if u < GH:
                    to, high = wq_l[:, u].rearrange("p c n -> p (c n)"), wq_h[:, u].rearrange("p c n -> p (c n)")
                else:
                    to, high = wo_l[:, i, u - GH, :], wo_h[:, i, u - GH, :]
                nc.gpsimd.tensor_tensor(to, piece, as_read(high), ALU.subtract).then_inc(ring_l, 1)

            def rotary_sum(m, half, head, i):
                pool.wait_ge(rope_ab, ONE + m + 1)
                nc.gpsimd.tensor_tensor(Q[:, head, half * HALF_TOK:(half + 1) * HALF_TOK], ra[:, i], rb[:, i],
                                        ALU.add).then_inc(q_ready, 1)

            for u in range(8):
                split_low(0, 0, u)
            for m in range(LEAD):
                rotary_sum(m, *PIECES[m], m % 2)
            for u in range(2):
                normalise(u, CROSS0 + u, CROSS0 + u - 1)

            def group(g, i, last):
                for b in range(NB):
                    n = CROSS0 + g * NU + b
                    if b + 2 < NB or not last:
                        normalise(b % 2, n + 2, n + 1)
                    if not last:
                        split_low(g + 1, 1 - i, b)
                    ahead, k = piece_at(b)
                    if not (ahead and last):
                        half, head = PIECES[k]
                        pool.wait_ge(s_ready, ONE + CROSS0 + (g + ahead - 1) * NU + half * 4 + 4)
                        rotary_sum(g * 8 + LEAD + b, half, head, b % 2)

            with pool.Fori(0, NG // 2 - 1) as g2:
                for i in range(2):
                    group(g2 * 2 + i, i, False)
            group(NG - 2, 0, False)
            group(NG - 1, 1, True)

        @block.scalar
        def _(act):
            for started in (xnT_hs, cxT_hs, v_taken, v_ready, vx_ready, qT_hs, kT_hs, kxT_ready, exp_done, pT_ready,
                            at_ready, oT_hs, ring_h):
                act.sem_inc(started, ONE)

            def spread_of(n):
                act.wait_ge(mv_done, n * NB + NB)
                nc.scalar.activation(spread[:], mean_var[:, :, 1], ACT.Sqrt, bias=eps[:, 0:1])\
                    .then_inc(spread_done, 1)
                nc.scalar.activation(unused[:], eps[:], ACT.Exp)

            def exponentials(i, n, used):
                act.wait_ge(masked, ONE + n + 1)
                act.wait_ge(prob_ready, ONE + used)
                for h in range(UH):
                    last = nc.scalar.activation(exps[:, i, h, :], neg_scores[:, i, h, :], ACT.Exp,
                                                bias=neg_max[:, i, h:h + 1], scale=-1.0,
                                                accum_out=sums[:, i, h:h + 1])
                last.then_inc(exp_done, 1)

            def take_probsT(i, n, used, ps):
                act.wait_ge(pT_ps, ONE + n + 1)
                act.wait_ge(av_done, ONE + used)
                nc.scalar.copy(probsT[:, i], ps[:].rearrange("p (h q) -> p h q", h=UH)).then_inc(pT_ready, 1)

            def split_high1(ks):
                for k in ks:
                    act.wait_ge(weight_in[k], 16 * len(weights1[k][2]))
                    nc.scalar.copy(weights1[k][0], loaded(k)).then_inc(weight_h, 1)

            def take_xnT(r):
                act.wait_ge(xnT_ps, ONE + r + 1)
                act.wait_ge(kv_ps, ONE + r)
                nc.scalar.copy(xnT_h[:], bank[7][:].rearrange("p (c t) -> p c t", c=EC)).then_inc(xnT_hs, 1)

            def take_v(r):
                act.wait_ge(kv_ps, ONE + r + 1)
                act.wait_ge(kab_done, ONE + r + 1)
                act.wait_ge(v_ready, ONE + r)
                nc.scalar.copy(vs[:], bank[6][:, P:2 * P]).then_inc(v_taken, 1)

            def place_v(r):
                act.wait_ge(v_taken, ONE + r + 1)
                act.wait_ge(av_done, ONE + r * NU)
                nc.scalar.copy(vz[:].rearrange("p (g c) -> p g c", c=VZ)[:, :, 0:SD],
                               vs[:].rearrange("p (g d) -> p g d", d=SD)).then_inc(v_ready, 1)

            def take_kT(r):
                act.wait_ge(kT_ps, ONE + r + 1)
                act.wait_ge(kTz_hs, ONE + r)
                nc.scalar.copy(kT_h[:], bank[6][:, 0:P]).then_inc(kT_hs, 1)

            def take_qT(r):
                act.wait_ge(qT_ps, ONE + r + 1)
                act.wait_ge(s_ready, ONE + r * NU)
                nc.scalar.copy(qT_h[:], bank[7][:].rearrange("p (j t) -> p j t", j=GH)).then_inc(qT_hs, 1)

            def take_cxT(r):
                act.wait_ge(cxT_ps, ONE + r + 1)
                act.wait_ge(vx_ps, ONE + 2 * r)
                nc.scalar.copy(cxT_h[:], bank[5][:].rearrange("p (c t) -> p c t", c=EC)).then_inc(cxT_hs, 1)

            def take_kxT(r, i):
                act.wait_ge(kxT_ps, ONE + 2 * r + i + 1)
                act.wait_ge(kv_stored, STORE_ONE + 32 * r)
                nc.scalar.copy(kxT[:, 4 * i:4 * i + 4, :], bank[5 + i][:].rearrange("p (g t) -> p g t", g=4))\
                    .then_inc(kxT_ready, 1)

            def take_vx(r, i):
                act.wait_ge(vx_ps, ONE + 2 * r + i + 1)
                nc.scalar.copy(vx[:, i * 512:(i + 1) * 512], bank[5][:]).then_inc(vx_ready, 1)

            def take_attention(r):
                act.wait_ge(av_done, ONE + r * NU + NU)
                act.wait_ge(o_ps, ONE + r)
                nc.scalar.copy(atT[:], bank[4][:].rearrange("p (j t) -> p j t", j=GH)).then_inc(at_ready, 1)

            def self_slot(r, u, last):
                n = r * NU + u
                take_probsT(u % 2, n, r * NU + max(u - 1, 0), bank[2 + u % 2])
                if u == 6 and not last:
                    take_qT(r + 1)
                if u == 7:
                    take_attention(r)
                if not last or u + 1 < NU:
                    exponentials((u + 1) % 2, n + 1, n)
                if u == 1 and not last:
                    take_xnT(r + 1)
                if u == 3:
                    if not last:
                        take_v(r + 1)
                    take_kxT(r, 0)
                if u == 4:
                    if not last:
                        take_kT(r + 1)
                    take_vx(r, 0)
                if u == 5:
                    take_kxT(r, 1)
                if u == 6:
                    take_vx(r, 1)
                if u == 7 and not last:
                    place_v(r + 1)
                    take_cxT(r + 1)

            act.wait_ge(eps_set, 1)
            spread_of(0)
            take_cxT(0)
            split_high1(SELF_W[0:2])
            take_xnT(0)
            split_high1(SELF_W[2:3])
            split_high1(KEY_W)
            take_v(0)
            take_kT(0)
            take_qT(0)
            act.wait_ge(vz_zero, 1)
            place_v(0)
            split_high1(VALUE_W[0:2])
            exponentials(0, 0, 0)
            split_high1(VALUE_W[2:4])
            self_slot(0, 0, False)
            act.wait_ge(v_weight_l, len(VALUE_W))
            with act.Fori(0, NB - 1) as r:
                for u in range(1, NU):
                    self_slot(r, u, False)
                self_slot(r + 1, 0, False)
            for u in range(1, NU):
                self_slot(NB - 1, u, True)

            act.wait_ge(x1_ready, ONE + NB)
            act.wait_ge(kv_stored, STORE_ONE + 32 * NB)

            def split_high(g, i, u):
                piece = ring[:, u % RING, :]
                act.wait_ge(ring_in[u % RING], 32 * g + 16 * (u // RING + 1))
                if u < GH:
                    to = wq_h[:, u].rearrange("p c n -> p (c n)")
                    act.wait_ge(qp_done, ONE + g * 8 - 8 + 5 + u if not isinstance(g, int) or g else ONE)
                else:
                    to = wo_h[:, i, u - GH, :]
                    act.wait_ge(y_done, ONE + g * NU - NU if not isinstance(g, int) or g else ONE)
                nc.scalar.copy(to, piece).then_inc(ring_h, 1)

            spread_of(1)
            for u in range(8):
                split_high(0, 0, u)
            for b in range(NB):
                act.wait_ge(xn2T_ps, b + 1)
                nc.scalar.copy(xn2T_h[:, :, b * P:(b + 1) * P], bank[2 + b % 2][:].rearrange("p (c t) -> p c t", c=EC))\
                    .then_inc(xn2T_hs, 1)
                act.wait_ge(tab_ps, b + 1)
                nc.scalar.copy(cosT[:, b * P:(b + 1) * P], bank[b % 2][:, 0:P])
                nc.scalar.copy(sinT[:, b * P:(b + 1) * P], bank[b % 2][:, P:2 * P]).then_inc(tab_ready, 1)
            for u in range(2):
                exponentials(u, CROSS0 + u, CROSS0 + u - 1)

            def group(g, i, last):
                for b in range(NB):
                    n = CROSS0 + g * NU + b
                    take_probsT(b % 2, n, n - 1, bank[4 + b % 2])
                    act.wait_ge(av_done, ONE + n + 1)
                    act.wait_ge(y_done, ONE + g * NU + b)
                    nc.scalar.copy(oT_h[:], bank[6][:].rearrange("p (h q) -> p h q", h=GH)).then_inc(oT_hs, 1)
                    if b + 2 < NB or not last:
                        exponentials(b % 2, n + 2, n + 1)
                    if not last:
                        split_high(g + 1, 1 - i, b)

            with act.Fori(0, NG // 2 - 1) as g2:
                for i in range(2):
                    group(g2 * 2 + i, i, False)
            group(NG - 2, 0, False)
            group(NG - 1, 1, True)
            spread_of(2)
            act.wait_ge(acc_done, ONE + NG * NU)
            act.wait_ge(rwT_ps, 1)
            nc.scalar.copy(rwT[:], bank[7][:, 0:EC * NE].rearrange("p (c n) -> p c n", c=EC)).then_inc(rwT_ready, 1)
            for b in range(NB):
                act.wait_ge(xn3T_ps, b + 1)
                nc.scalar.copy(xn3T[:, :, b * P:(b + 1) * P], bank[b % 4][:].rearrange("p (c t) -> p c t", c=EC))\
                    .then_inc(xn3T_ready, 1)
            act.wait_ge(ffn_step, 3)
            nc.scalar.activation(lex[:], lsh[:], ACT.Exp).then_inc(lex_done, 1)
            for h in range(2):
                act.wait_ge(wdT_ps, h + 1)
                nc.scalar.copy(wdT[:, h * 512:(h + 1) * 512], bank[4 + h][0:NE, :]).then_inc(wdT_ready, 1)

        @block.vector
        def _(dve):
            for started in (xn_ready, xnT_ls, cxT_ls, qab_done, kab_done, kr_ready, kxab_done, kT_ls, kTz_ls, qT_ls,
                            masked, rsum_ready, x1_ready, rope_ab, oT_ls, acc_done):
                dve.sem_inc(started, ONE)
            nc.vector.memset(eps[:], EPS).then_inc(eps_set, 1)

            def statistics(b, n):
                nc.vector.bn_stats(stats[:, 0, :], row(X, b)).then_inc(stats_done, 1)
                dve.wait_ge(stats_done, n + 1)
                dve.sem_inc(dve_passed)
                nc.vector.bn_aggr(one_row[:], stats[:, 0, :]).then_inc(aggr_done, 1)
                dve.wait_ge(aggr_done, n - NB + 1)
                dve.sem_inc(dve_passed)
                nc.vector.tensor_copy(row(mean_var, b), one_row[:]).then_inc(mv_done, 1)
                dve.wait_ge(mv_done, n + 1)

            def invert_spread(n):
                dve.wait_ge(spread_done, n + 1)
                nc.vector.reciprocal(rstd[:], spread[:]).then_inc(rstd_done, 1)
                dve.wait_ge(rstd_done, n + 1)

            def normed(to, b):
                return nc.vector.tensor_scalar(to, row(X, b), row(mean_var, b)[:, 0:1], rstd[:, bass.ds(b, 1)],
                                               ALU.subtract, ALU.mult)

            def mask_scores(i, n, used, ps, added, scale):
                dve.wait_ge(s_ready, ONE + n + 1)
                dve.wait_ge(exp_done, ONE + used)
                dve.sem_inc(dve_passed)
                for h in range(UH):
                    last = nc.vector.tensor_tensor_reduce(
                        out=neg_scores[:, i, h, :], in0=ps[:, h * P:(h + 1) * P], in1=added, scale=-scale,
                        scalar=BIG, op0=ALU.add, op1=ALU.min, accum_out=neg_max[:, i, h:h + 1])
                last.then_inc(masked, 1)

            def invert_sums(i, n):
                dve.wait_ge(exp_done, ONE + n + 1)
                nc.vector.reciprocal(rsums[:, i], sums[:, i]).then_inc(rsum_ready, 1)

            def rotate(to_a, to_b, src, heads, width, cos, sin_low, sin_high):
                half = width // 2
                v, a, b_ = (t.rearrange("p (h d) -> p h d", d=width) for t in (src, to_a, to_b))
                nc.vector.tensor_tensor(a, v, cos.unsqueeze(1).to_broadcast([P, heads, width]), ALU.mult)
                nc.vector.tensor_tensor(b_[:, :, 0:half], v[:, :, half:width],
                                        sin_low.unsqueeze(1).to_broadcast([P, heads, half]), ALU.mult)
                return nc.vector.tensor_tensor(b_[:, :, half:width], v[:, :, 0:half],
                                               sin_high.unsqueeze(1).to_broadcast([P, heads, half]), ALU.mult)

            def low(to, ps, high):
                return nc.vector.tensor_tensor(to, ps, as_read(high), ALU.subtract)

            def split_low1(ks):
                for k in ks:
                    dve.wait_ge(weight_h, k + 1)
                    high, part = weights1[k][0:2]
                    low(part, loaded(k), high).then_inc(weight_l, 1)

            def norm_row(r):
                dve.wait_ge(xnT_ps, ONE + r)
                normed(xn[:], r).then_inc(xn_ready, 1)

            def low_xnT(r):
                dve.wait_ge(xnT_hs, ONE + r + 1)
                low(xnT_l[:], bank[7][:].rearrange("p (c t) -> p c t", c=EC), xnT_h[:]).then_inc(xnT_ls, 1)

            def low_cxT(r):
                dve.wait_ge(cxT_hs, ONE + r + 1)
                low(cxT_l[:], bank[5][:].rearrange("p (c t) -> p c t", c=EC), cxT_h[:]).then_inc(cxT_ls, 1)

            def rotate_q(r):
                dve.wait_ge(q_ps, ONE + r + 1)
                dve.wait_ge(qr_ready, ONE + r)
                rotate(qa[:], qb[:], bank[7][:], E // SD, SD, rope_s[:, 0:SD], rope_s[:, SD:SD + 8],
                       rope_s[:, SD + 8:2 * SD]).then_inc(qab_done, 1)

            def rotate_k(r):
                dve.wait_ge(kv_ps, ONE + r + 1)
                dve.wait_ge(kr_ready, ONE + r)
                rotate(ka[:], kb[:], bank[6][:, 0:P], NG, SD, rope_s[:, 0:SD], rope_s[:, SD:SD + 8],
                       rope_s[:, SD + 8:2 * SD]).then_inc(kab_done, 1)
                dve.wait_ge(kab_done, ONE + r + 1)
                dve.wait_ge(kT_ps, ONE + r)
                nc.vector.tensor_tensor(kr[:], ka[:], kb[:], ALU.add).then_inc(kr_ready, 1)

            def rotate_kx(r, i):
                dve.wait_ge(kx_ps, ONE + 2 * r + i + 1)
                dve.wait_ge(kxr_ready, ONE + 2 * r + i)
                tab = row(rope_x, r)
                rotate(kxa[:], kxb[:], bank[5 + i][:], 4, XD, tab[:, 0:128], tab[:, 192:256], tab[:, 128:192])\
                    .then_inc(kxab_done, 1)

            def low_kT(r):
                dve.wait_ge(kT_hs, ONE + r + 1)
                dve.wait_ge(kTz_ls, ONE + r)
                low(kT_l[:], bank[6][:, 0:P], kT_h[:]).then_inc(kT_ls, 1)

            def spread_keys_low(r):
                dve.wait_ge(kT_ls, ONE + r + 1)
                dve.wait_ge(s_ready, ONE + r * NU)
                nc.vector.tensor_tensor(kTz_l[:], kT_l[:].unsqueeze(1).to_broadcast([P, NG, P]),
                                        rows[:].unsqueeze(2).to_broadcast([P, NG, P]), ALU.mult).then_inc(kTz_ls, 1)

            def low_qT(r):
                dve.wait_ge(qT_hs, ONE + r + 1)
                low(qT_l[:], bank[7][:].rearrange("p (j t) -> p j t", j=GH), qT_h[:]).then_inc(qT_ls, 1)

            def add_attention(r):
                dve.wait_ge(o_ps, ONE + r + 1)
                nc.vector.tensor_tensor(row(X, r), bank[7][:], row(X, r), ALU.add).then_inc(x1_ready, 1)
                dve.wait_ge(x1_ready, ONE + r + 1)
                dve.sem_inc(dve_passed)
                statistics(r, r + NB)

            def self_slot(r, u, last, first=False):
                n = r * NU + u
                if not last or u + 1 < NU:
                    mask_scores((u + 1) % 2, n + 1, n, bank[(u + 1) % 2], causal[:], SELF_SCALE)
                if u == 0 and not first:
                    add_attention(r - 1)
                if u == 1 and not last:
                    norm_row(r + 1)
                if u == 6 and not last:
                    low_qT(r + 1)
                    spread_keys_low(r + 1)
                if not last or u + 1 < NU:
                    invert_sums((u + 1) % 2, n + 1)
                if u < 2:
                    rotate_kx(r, u)
                if not last:
                    if u == 1:
                        low_xnT(r + 1)
                    if u == 2:
                        rotate_q(r + 1)
                    if u == 3:
                        rotate_k(r + 1)
                    if u == 4:
                        low_kT(r + 1)
                    if u == 7:
                        low_cxT(r + 1)

            dve.wait_ge(pos_in, 16)
            nc.vector.tensor_scalar(posf[:], posi[:], 0.0, float(MAXPOS), ALU.is_lt, ALU.mult).then_inc(pos_a, 1)
            dve.wait_ge(pos_a, 1)
            nc.vector.tensor_tensor(posn[:], posi[:], posf[:], ALU.add).then_inc(pos_b, 1)
            dve.wait_ge(pos_b, 1)
            nc.vector.tensor_scalar(posu[:], posn[:], 0.0, float(MAXPOS - 1), ALU.max, ALU.min).then_inc(pos_ready, 1)
            for b in range(NB):
                dve.wait_ge(x_in[b], 16)
                nc.vector.bn_stats(stats[:, b, :], X[:, b, :]).then_inc(stats_done, 1)
            dve.wait_ge(stats_done, NB)
            for b in range(NB):
                nc.vector.bn_aggr(mean_var[:, b, :], stats[:, b, :]).then_inc(mv_done, 1)
            dve.wait_ge(mv_done, NB)
            low_cxT(0)
            invert_spread(0)
            norm_row(0)
            split_low1(SELF_W[0:2])
            low_xnT(0)
            split_low1(SELF_W[2:3])
            split_low1(KEY_W[0:2])
            dve.wait_ge(small_in, 48)
            rotate_q(0)
            rotate_k(0)
            low_kT(0)
            spread_keys_low(0)
            low_qT(0)
            mask_scores(0, 0, 0, bank[0], causal[:], SELF_SCALE)
            split_low1(KEY_W[2:4])
            invert_sums(0, 0)
            dve.wait_ge(gathered, 16 * NB)
            self_slot(0, 0, False, first=True)
            with dve.Fori(0, NB - 1) as r:
                for u in range(1, NU):
                    self_slot(r, u, False)
                self_slot(r + 1, 0, False)
            for u in range(1, NU):
                self_slot(NB - 1, u, True)
            add_attention(NB - 1)

            dve.wait_ge(kv_stored, STORE_ONE + 32 * NB)
            invert_spread(1)
            for b in range(NB):
                if b >= 2:
                    dve.wait_ge(xn2T_ps, b - 1)
                normed(xn2[:, b % 2], b).then_inc(xn2_ready, 1)
                if b:
                    dve.wait_ge(xn2T_hs, b)
                    t = slice((b - 1) * P, b * P)
                    low(xn2T_l[:, :, t], bank[2 + (b - 1) % 2][:].rearrange("p (c t) -> p c t", c=EC), xn2T_h[:, :, t])\
                        .then_inc(xn2T_ls, 1)
            dve.wait_ge(xn2T_hs, NB)
            low(xn2T_l[:, :, (NB - 1) * P:], bank[3][:].rearrange("p (c t) -> p c t", c=EC), xn2T_h[:, :, (NB - 1) * P:])\
                .then_inc(xn2T_ls, 1)
            dve.wait_ge(mask_in, 16)
            nc.vector.tensor_scalar(bias[:], maski[:], 0.0, NEG, ALU.is_equal, ALU.mult).then_inc(bias_ready, 1)
            dve.wait_ge(bias_ready, 1)
            dve.wait_ge(tab_ready, NB)

            def rotate_piece(m, half, i, summed):
                dve.wait_ge(qp_done, ONE + m + 1)
                dve.wait_ge(q_ready, ONE + summed)
                t = slice(half * HALF_TOK, (half + 1) * HALF_TOK)
                lo, hi = slice(0, XD // 2), slice(XD // 2, XD)
                nc.vector.tensor_tensor(ra[:, i], bank[i][:], cosT[:, t], ALU.mult)
                nc.vector.tensor_tensor(rb[lo, i], bank[i][hi, :], sinT[hi, t], ALU.mult)
                nc.vector.tensor_tensor(rb[hi, i], bank[i][lo, :], sinT[lo, t], ALU.mult).then_inc(rope_ab, 1)

            for m in range(LEAD):
                rotate_piece(m, PIECES[m][0], m % 2, max(m - 1, 0))
            for u in range(2):
                mask_scores(u, CROSS0 + u, CROSS0 + u - 1, bank[2 + u], bias[:, u, :], CROSS_SCALE)
                invert_sums(u, CROSS0 + u)

            def group(g, last):
                for b in range(NB):
                    n = CROSS0 + g * NU + b
                    if b + 2 < NB or not last:
                        mask_scores(b % 2, n + 2, n + 1, bank[2 + b % 2], bias[:, (b + 2) % NB, :], CROSS_SCALE)
                    dve.wait_ge(oT_hs, ONE + g * NU + b + 1)
                    dve.wait_ge(y_done, ONE + g * NU + b)
                    low(oT_l[:], bank[6][:].rearrange("p (h q) -> p h q", h=GH), oT_h[:]).then_inc(oT_ls, 1)
                    if b + 2 < NB or not last:
                        invert_sums(b % 2, n + 2)
                    ahead, k = piece_at(b)
                    if not (ahead and last):
                        m = g * 8 + LEAD + b
                        rotate_piece(m, PIECES[k][0], b % 2, m - 1)
                    dve.wait_ge(y_done, ONE + g * NU + b + 1)
                    dve.wait_ge(acc_done, ONE + g * NU + b)
                    nc.vector.tensor_tensor(X[:, b, :], bank[7][:], X[:, b, :], ALU.add).then_inc(acc_done, 1)
                    if last:
                        dve.wait_ge(acc_done, ONE + g * NU + b + 1)
                        statistics(b, 2 * NB + b)

            with dve.Fori(0, NG // 2 - 1) as g2:
                for i in range(2):
                    group(g2 * 2 + i, False)
            group(NG - 2, False)
            group(NG - 1, True)

            invert_spread(2)
            for b in range(NB):
                normed(xn3[:, b, :], b).then_inc(xn3_ready, 1)
            dve.wait_ge(ffn_in, 48)
            dve.wait_ge(lg_ps, 1)

            steps = [0]

            def step(ins):
                steps[0] += 1
                ins.then_inc(ffn_step, 1)
                dve.wait_ge(ffn_step, steps[0])

            wide = [P, NB, NE]
            step(nc.vector.tensor_tensor(lg[:], bank[6][:].rearrange("p (b n) -> p b n", b=NB),
                                         rb_row[:].unsqueeze(1).to_broadcast(wide), ALU.add))
            step(nc.vector.tensor_reduce(lmax[:], lg[:], AX.X, ALU.max))
            step(nc.vector.tensor_tensor(lsh[:], lg[:], lmax[:].unsqueeze(2).to_broadcast(wide), ALU.subtract))
            dve.wait_ge(lex_done, 1)
            step(nc.vector.tensor_reduce(lsum[:], lex[:], AX.X, ALU.add))
            step(nc.vector.reciprocal(lrs[:], lsum[:]))
            step(nc.vector.tensor_tensor(lsc[:], lex[:], lrs[:].unsqueeze(2).to_broadcast(wide), ALU.mult))
            for b in range(NB):
                last = nc.vector.max(top[:, b, :], lsc[:, b, :])
            step(last)
            for b in range(NB):
                last = nc.vector.match_replace(out=cut[:, b, :], in_to_replace=top[:, b, :],
                                               in_values=lsc[:, b, :], imm_value=-1.0)
            step(last)
            step(nc.vector.scalar_tensor_tensor(out=wd[:], in0=cut[:], scalar=0.0, in1=lsc[:], op0=ALU.is_lt,
                                                op1=ALU.mult))
            step(nc.vector.tensor_reduce(wsum[:], wd[:], AX.X, ALU.add))
            for b in range(NB):
                last = nc.vector.scalar_tensor_tensor(out=X[:, b, :], in0=xn3[:, b, :], scalar=wsum[:, b:b + 1],
                                                      in1=X[:, b, :], op0=ALU.mult, op1=ALU.add)
            step(last)
            for b in range(NB):
                dve.wait_ge(mix_ps, b + 1)
                nc.vector.tensor_tensor(xn3[:, b, :], bank[b % 4][:], X[:, b, :], ALU.add).then_inc(fin_ready, 1)

        @block.tensor
        def _(pe):
            for started in (xnT_ps, cxT_ps, q_ps, kv_ps, kx_ps, vx_ps, qT_ps, kT_ps, kxT_ps, o_ps, s_ready, pT_ps,
                            av_done, qp_done, y_done):
                pe.sem_inc(started, ONE)

            def transpose_chunks(ps, src, n=4):
                for c in range(n):
                    last = nc.tensor.transpose(ps[:, c * P:(c + 1) * P], src[:, c * P:(c + 1) * P], ident[:])
                return last

            def product(ps, lhsT, rhs):
                for c in range(EC):
                    last = nc.tensor.matmul(ps, lhsT(c), rhs(c), start=(c == 0), stop=(c == EC - 1))
                return last

            def product3(ps, terms):
                for t, (a_h, a_l, b_h, b_l) in enumerate(terms):
                    nc.tensor.matmul(ps, a_h, b_l, start=(t == 0), stop=False)
                    nc.tensor.matmul(ps, a_h, b_h, start=False, stop=False)
                    last = nc.tensor.matmul(ps, a_l, b_h, start=False, stop=(t == len(terms) - 1))
                return last

            def transpose_probs(i, n, ps):
                pe.wait_ge(prob_ready, ONE + n + 1)
                for h in range(UH):
                    last = nc.tensor.transpose(ps[:, h * P:(h + 1) * P], probs[:, i, h, :], ident[:])
                last.then_inc(pT_ps, 1)

            def turn_context(r):
                pe.wait_ge(ctx_in_, 16 * r + 16)
                pe.wait_ge(vx_ready, ONE + 2 * r)
                transpose_chunks(bank[5], cx).then_inc(cxT_ps, 1)

            def turn_x(r, added):
                pe.wait_ge(xn_ready, ONE + r + 1)
                pe.wait_ge(x1_ready, ONE + added)
                transpose_chunks(bank[7], xn).then_inc(xnT_ps, 1)

            def make_q(r):
                pe.wait_ge(xnT_hs, ONE + r + 1)
                pe.wait_ge(xnT_ls, ONE + r + 1)
                product3(bank[7][:], [(xnT_h[:, c, :], xnT_l[:, c, :], wq1_h[:, c, :], wq1_l[:, c, :])
                                      for c in range(EC)]).then_inc(q_ps, 1)

            def make_kv(r):
                pe.wait_ge(kxab_done, ONE + 2 * r)
                product3(bank[6][:, 0:2 * P], [(xnT_h[:, c, :], xnT_l[:, c, :], wkv1_h[:, c, :], wkv1_l[:, c, :])
                                               for c in range(EC)]).then_inc(kv_ps, 1)

            def turn_k(r):
                pe.wait_ge(kr_ready, ONE + r + 1)
                pe.wait_ge(v_taken, ONE + r + 1)
                nc.tensor.transpose(bank[6][:, 0:P], kr[:], ident[:]).then_inc(kT_ps, 1)

            def turn_q(r):
                pe.wait_ge(qr_ready, ONE + r + 1)
                transpose_chunks(bank[7], qr).then_inc(qT_ps, 1)

            def make_kx(r, i):
                if i == 0:
                    pe.wait_ge(cxT_hs, ONE + r + 1)
                    pe.wait_ge(cxT_ls, ONE + r + 1)
                else:
                    pe.wait_ge(kT_ls, ONE + r + 1)
                    pe.wait_ge(kxT_ready, ONE + 2 * r)
                n = slice(i * 512, (i + 1) * 512)
                product3(bank[5 + i][:], [(cxT_h[:, c, :], cxT_l[:, c, :], wk2_h[:, c, n], wk2_l[:, c, n])
                                          for c in range(EC)]).then_inc(kx_ps, 1)

            def make_vx(r, i):
                if i == 0:
                    pe.wait_ge(kxT_ready, ONE + 2 * r + 1)
                else:
                    pe.wait_ge(vx_ready, ONE + 2 * r + 1)
                n = slice(i * 512, (i + 1) * 512)
                product3(bank[5][:], [(cxT_h[:, c, :], cxT_l[:, c, :], wv2_h[:, c, n], wv2_l[:, c, n])
                                      for c in range(EC)]).then_inc(vx_ps, 1)

            def turn_kx(r, i):
                pe.wait_ge(kxr_ready, ONE + 2 * r + i + 1)
                transpose_chunks(bank[5 + i], kxr[:, i]).then_inc(kxT_ps, 1)

            def scores(u):
                j, g = u // 2, slice(4 * (u % 2), 4 * (u % 2) + 4)
                product3(bank[u % 2][:], [(qT_h[:, j, :], qT_l[:, j, :], kTz_h[:, g, :], kTz_l[:, g, :])])\
                    .then_inc(s_ready, 1)

            def wait_for_row(r):
                for ready in (qT_hs, qT_ls, kTz_hs, kTz_ls):
                    pe.wait_ge(ready, ONE + r + 1)

            def self_slot(r, u, last):
                n = r * NU + u
                pe.wait_ge(pT_ready, ONE + r * NU + max(u - 1, 0))
                transpose_probs(u % 2, n, bank[2 + u % 2])
                if u == 0:
                    make_kx(r, 0)
                if u == 1:
                    make_kx(r, 1)
                    if not last:
                        turn_x(r + 1, r)
                if u == 2 and not last:
                    make_q(r + 1)
                if u == 3:
                    if not last:
                        make_kv(r + 1)
                    turn_kx(r, 0)
                if u == 4:
                    if not last:
                        turn_k(r + 1)
                    make_vx(r, 0)
                if u == 5:
                    if not last:
                        pe.wait_ge(kT_ls, ONE + r + 2)
                    turn_kx(r, 1)
                    if not last:
                        turn_q(r + 1)
                if u == 6:
                    make_vx(r, 1)
                if u == 7 and not last:
                    turn_context(r + 1)
                pe.wait_ge(pT_ready, ONE + n + 1)
                if u == 0:
                    pe.wait_ge(v_ready, ONE + r + 1)
                    pe.wait_ge(at_ready, ONE + r)
                j, half = u // 2, u % 2
                for i in range(UH):
                    g = UH * half + i
                    done = nc.tensor.matmul(bank[4][:, j * P:(j + 1) * P], vz[:, g * P:(g + 1) * P],
                                            probsT[:, u % 2, i, :], start=(g == 0), stop=(g == NG - 1))
                done.then_inc(av_done, 1)
                if not last or u + 2 < NU:
                    pe.wait_ge(masked, ONE + n + 1)
                    if u == 6:
                        wait_for_row(r + 1)
                    scores((u + 2) % NU)
                if u == 7:
                    pe.wait_ge(at_ready, ONE + r + 1)
                    for j in range(GH):
                        done = nc.tensor.matmul(bank[7][:], atT[:, j, :], wo1[:, j, :], start=(j == 0),
                                                stop=(j == GH - 1))
                    done.then_inc(o_ps, 1)

            pe.wait_ge(ident_in, 16)
            turn_context(0)
            turn_x(0, 0)
            pe.wait_ge(weight_l, 2)
            make_q(0)
            pe.wait_ge(weight_l, len(SELF_W))
            make_kv(0)
            turn_k(0)
            turn_q(0)
            wait_for_row(0)
            for u in range(2):
                scores(u)
            pe.wait_ge(weight_l, len(SELF_W) + len(KEY_W))
            self_slot(0, 0, False)
            pe.wait_ge(v_weight_l, len(VALUE_W))
            pe.wait_ge(wo1_in, 16 * NG)
            with pe.Fori(0, NB - 1) as r:
                for u in range(1, NU):
                    self_slot(r, u, False)
                self_slot(r + 1, 0, False)
            for u in range(1, NU):
                self_slot(NB - 1, u, True)

            pe.wait_ge(x1_ready, ONE + NB)
            pe.wait_ge(gathered, 16 * NB)
            for b in range(NB):
                if b >= 2:
                    pe.wait_ge(xn2T_ls, b - 1)
                pe.wait_ge(xn2_ready, b + 1)
                transpose_chunks(bank[2 + b % 2], xn2[:, b % 2]).then_inc(xn2T_ps, 1)
                if b >= 2:
                    pe.wait_ge(tab_ready, b - 1)
                for i in range(2):
                    last = nc.tensor.transpose(bank[b % 2][:, i * P:(i + 1) * P], rope_x[:, b, i * P:(i + 1) * P],
                                               ident[:])
                last.then_inc(tab_ps, 1)
            pe.wait_ge(tab_ready, NB)
            pe.wait_ge(xn2T_ls, NB)

            def make_piece(m, g, half, head, i, rotated):
                pe.wait_ge(ring_l, ONE + g * 8 + head + 1)
                pe.wait_ge(rope_ab, ONE + rotated)
                t = slice(half * HALF_TOK, (half + 1) * HALF_TOK)
                product3(bank[i][:], [(wq_h[:, head, c, :], wq_l[:, head, c, :], xn2T_h[:, c, t], xn2T_l[:, c, t])
                                      for c in range(EC)]).then_inc(qp_done, 1)

            def cross_scores(n, g, b, i):
                pe.wait_ge(masked, ONE + n - 1)
                pe.wait_ge(kv_in, 32 * (g + 1))
                pe.wait_ge(q_ready, ONE + g * 8 + (b // 4) * 4 + 4)
                for h in range(GH):
                    last = nc.tensor.matmul(bank[2 + b % 2][:, h * P:(h + 1) * P], Q[:, h, b * P:(b + 1) * P],
                                            k_g[:, i, b * P:(b + 1) * P], start=True, stop=True)
                last.then_inc(s_ready, 1)

            for m in range(LEAD):
                make_piece(m, 0, *PIECES[m], m % 2, max(m - 1, 0))
            for b in range(2):
                cross_scores(CROSS0 + b, 0, b, 0)

            def group(g, i, last_group):
                for b in range(NB):
                    n = CROSS0 + g * NU + b
                    pe.wait_ge(pT_ready, ONE + n - 1)
                    transpose_probs(b % 2, n, bank[4 + b % 2])
                    if b + 2 < NB:
                        cross_scores(n + 2, g, b + 2, i)
                    elif not last_group:
                        cross_scores(n + 2, g + 1, b + 2 - NB, 1 - i)
                    pe.wait_ge(pT_ready, ONE + n + 1)
                    pe.wait_ge(oT_ls, ONE + g * NU + b)
                    nc.tensor.matmul(bank[6][:], v_g[:, i, b, :], probsT[:, b % 2], start=True, stop=True)\
                        .then_inc(av_done, 1)
                    ahead, k = piece_at(b)
                    if not (ahead and last_group):
                        half, head = PIECES[k]
                        m = g * 8 + LEAD + b
                        make_piece(m, g + ahead, half, head, b % 2, m - 1)
                    pe.wait_ge(ring_l, ONE + (g + 1) * 8)
                    pe.wait_ge(oT_ls, ONE + g * NU + b + 1)
                    pe.wait_ge(acc_done, ONE + g * NU + b)
                    product3(bank[7][:], [(oT_h[:, h, :], oT_l[:, h, :], wo_h[:, i, h, :], wo_l[:, i, h, :])
                                          for h in range(GH)]).then_inc(y_done, 1)

            with pe.Fori(0, NG // 2 - 1) as g2:
                for i in range(2):
                    group(g2 * 2 + i, i, False)
            group(NG - 2, 0, False)
            group(NG - 1, 1, True)

            pe.wait_ge(ffn_in, 48)
            pe.wait_ge(acc_done, ONE + NG * NU)
            for c in range(EC):
                last = nc.tensor.transpose(bank[7][:, c * NE:(c + 1) * NE], rw[:, c * P:(c + 1) * P],
                                           ident[0:NE, 0:NE])
            last.then_inc(rwT_ps, 1)
            pe.wait_ge(oT_ls, ONE + NG * NU)
            for b in range(NB):
                if b >= 4:
                    pe.wait_ge(xn3T_ready, b - 3)
                pe.wait_ge(xn3_ready, b + 1)
                transpose_chunks(bank[b % 4], xn3[:, b, :]).then_inc(xn3T_ps, 1)
            pe.wait_ge(rwT_ready, 1)
            for b in range(NB):
                pe.wait_ge(xn3T_ready, b + 1)
                last = product(bank[6][:, b * NE:(b + 1) * NE], lambda c: xn3T[:, c, b * P:(b + 1) * P],
                               lambda c: rwT[:, c, :])
            last.then_inc(lg_ps, 1)
            pe.wait_ge(ffn_step, 9)
            for h in range(2):
                for k in range(4):
                    last = nc.tensor.transpose(bank[4 + h][0:NE, k * P:(k + 1) * P], wd[:, 4 * h + k, :], ident[:])
                last.then_inc(wdT_ps, 1)
            for b in range(NB):
                pe.wait_ge(wdT_ready, b // 4 + 1)
                if b >= 4:
                    pe.wait_ge(fin_ready, b - 3)
                nc.tensor.matmul(bank[b % 4][:], wdT[:, b * P:(b + 1) * P], eb[:], start=True, stop=True)\
                    .then_inc(mix_ps, 1)


def constants():
    import numpy as np

    f = np.float32
    steps = np.arange(P, dtype=f)
    inv = (f(1) / f(500000.0) ** (np.arange(0, SD, 2, dtype=f) / f(SD))).astype(f)
    angle = (steps[:, None] * inv[None, :]).astype(f)
    c, s = np.cos(angle), np.sin(angle)
    rope_self = np.concatenate([c, c, -s, s], 1).astype(f)
    inv = (f(1) / f(10000.0) ** (np.arange(0, XD, 2, dtype=f) / f(XD))).astype(f)
    angle = (np.arange(MAXPOS, dtype=f)[:, None] * inv[None, :]).astype(f)
    c, s = np.cos(angle), np.sin(angle)
    rope_cross = np.concatenate([c, c, s, -s], 1).astype(f)
    causal = np.where(np.triu(np.ones((P, P), bool), 1), f(NEG), f(0)).astype(f)
    rows = (np.arange(P)[:, None] // SD == np.arange(NG)[None, :]).astype(f)
    return {"c_ident": np.eye(P, dtype=f), "c_causal": causal, "c_rope_self": rope_self,
            "c_rope_cross": rope_cross, "c_rows": rows}


_INS = ["x", "ctx_4096", "pos_BxS2", "mask_BxSxS2_ik0", "L0_attn_Wq", "L0_attn_Wk", "L0_attn_Wv", "L0_attn_Wo",
        "L0_xattn_Wq", "L0_xattn_Wk", "L0_xattn_Wv", "L0_xattn_Wo", "L0_ffn_router_weight", "L0_ffn_router_bias",
        "L0_ffn_expert_bias"]


def kernel(**inputs):
    import numpy as _np
    import concourse.bacc as _bacc
    from concourse import mybir as _mybir
    from concourse.bass_utils import run_bass_kernel_spmd as _run

    nc = _bacc.Bacc("TRN2", target_bir_lowering=False, num_devices=1)
    arrays, args = {}, []
    for name, a in [(n, inputs[n]) for n in _INS] + list(constants().items()):
        a = _np.ascontiguousarray(_np.transpose(a) if name == "pos_BxS2" else a)
        arrays[f"in_{name}"] = a
        args.append(nc.dram_tensor(f"in_{name}", a.shape, _mybir.dt.from_np(a.dtype), kind="ExternalInput").ap())
    args.append(nc.dram_tensor("out_0", (NB, P, E), F32, kind="ExternalOutput").ap())
    decoder(nc, *args)
    r = _run(nc, [arrays], core_ids=[0])
    return r.results[0]["out_0"]
```

```python
from contextlib import ExitStack
import math

import concourse.bass as bass
from concourse import mybir

F32 = mybir.dt.float32
F32R = mybir.dt.float32r
I32 = mybir.dt.int32
U32 = mybir.dt.uint32
ALU = mybir.AluOpType
ACT = mybir.ActivationFunctionType
AX = mybir.AxisListType

P = 128
NB = 8
E = 512
EC = E // P
NU = 8
UH = 4
NG = 8
GH = 4
SD = 16
XD = 128
MAXPOS = 512
SELF_SCALE = 1.0 / math.sqrt(SD)
CROSS_SCALE = 1.0 / math.sqrt(XD)
NEG = -float(2 ** 100)
BIG = 3.0e38
EPS = 1e-5
NE = 64
TOP = 8
RING = 4
VZ = 9 * SD
HALF_TOK = 4 * P


def decoder(nc, x, ctx, pos, mask, wq_s, wk_s, wv_s, wo_s, wq_x, wk_x, wv_x, wo_x,
            router_w, router_b, expert_b, c_ident, c_causal, c_rope_self, c_rope_cross, c_rows, out):
    k_dram = nc.dram_tensor("k_cross", (NG, XD, NB * P), F32, kind="Internal").ap()
    v_dram = nc.dram_tensor("v_cross", (NB, P, NG * XD), F32, kind="Internal").ap()

    with ExitStack() as whole:
        def sem(name):
            return whole.enter_context(nc.semaphore(name))

        def keep(name, shape, dt=F32):
            return whole.enter_context(nc.sbuf_tensor(name, shape, dt))

        bank = [whole.enter_context(nc.psum_tensor(f"bank{i}", [P, 512], F32)) for i in range(8)]

        ident = keep("ident", [P, P])
        X = keep("X", [P, NB, E])
        rope_x = keep("rope_x", [P, NB, 4 * 64])
        mean_var = keep("mean_var", [P, NB, 2])
        stats = keep("stats", [P, NB, 6])
        one_row = keep("one_row", [P, 2])
        spread = keep("spread", [P, NB])
        rstd = keep("rstd", [P, NB])
        eps = keep("eps", [P, 1])
        unused = keep("unused", [P, 12])
        neg_scores = keep("neg_scores", [P, 2, UH, P])
        neg_max = keep("neg_max", [P, 2, UH])
        exps = keep("exps", [P, 2, UH, P])
        sums = keep("sums", [P, 2, UH])
        rsums = keep("rsums", [P, 2, UH])
        probs = keep("probs", [P, 2, UH, P])
        probsT = keep("probsT", [P, 2, UH, P])
        ring = keep("ring", [P, RING, 512])

        first = ExitStack()

        def one(name, shape, dt=F32):
            return first.enter_context(nc.sbuf_tensor(name, shape, dt))

        wq1_h, wq1_l = one("wq1_h", [P, EC, E], F32R), one("wq1_l", [P, EC, E], F32R)
        wkv1_h, wkv1_l = one("wkv1_h", [P, EC, 2 * P], F32R), one("wkv1_l", [P, EC, 2 * P], F32R)
        xn = one("xn", [P, E])
        xnT_h, xnT_l = one("xnT_h", [P, EC, P], F32R), one("xnT_l", [P, EC, P], F32R)
        qa = one("qa", [P, E])
        wk2_h, wk2_l = one("wk2_h", [P, EC, NG * XD], F32R), one("wk2_l", [P, EC, NG * XD], F32R)
        wv2_h, wv2_l = one("wv2_h", [P, EC, NG * XD], F32R), one("wv2_l", [P, EC, NG * XD], F32R)
        wo1 = one("wo1", [P, GH, E])
        causal = one("causal", [P, P])
        rope_s = one("rope_s", [P, 2 * SD])
        rows = one("rows", [P, NG])
        posi = one("posi", [P, NB], I32)
        posf = one("posf", [P, NB])
        posn = one("posn", [P, NB])
        posu = one("posu", [P, NB], U32)
        cx = one("cx", [P, E])
        cxT_h, cxT_l = one("cxT_h", [P, EC, P], F32R), one("cxT_l", [P, EC, P], F32R)
        qb = one("qb", [P, E])
        qr = one("qr", [P, E])
        ka = one("ka", [P, P])
        kb = one("kb", [P, P])
        kr = one("kr", [P, P])
        vs = one("vs", [P, P])
        kxa = one("kxa", [P, E])
        kxb = one("kxb", [P, E])
        kxr = one("kxr", [P, 2, E])
        kxT = one("kxT", [P, NG, P])
        vx = one("vx", [P, NG * XD])
        qT_h, qT_l = one("qT_h", [P, GH, P], F32R), one("qT_l", [P, GH, P], F32R)
        kT_h, kT_l = one("kT_h", [P, P], F32R), one("kT_l", [P, P])
        kTz_h, kTz_l = one("kTz_h", [P, NG, P], F32R), one("kTz_l", [P, NG, P], F32R)
        vz = one("vz", [P, NG * VZ])
        atT = one("atT", [P, GH, P])
        first.close()

        second = ExitStack()

        def two(name, shape, dt=F32):
            return second.enter_context(nc.sbuf_tensor(name, shape, dt))

        xn2T_h, xn2T_l = two("xn2T_h", [P, EC, NB * P], F32R), two("xn2T_l", [P, EC, NB * P], F32R)
        wq_h, wq_l = two("wq_h", [P, GH, EC, XD], F32R), two("wq_l", [P, GH, EC, XD], F32R)
        xn2 = two("xn2", [P, 2, E])
        table = two("table", [P, 2, NB * P])
        cosT, sinT = table[:, 0, :], table[:, 1, :]
        k_g = two("k_g", [P, 2, NB * P])
        v_in = two("v_in", [P, NB, XD])
        v_h, v_l = two("v_h", [P, 2, NB, XD], F32R), two("v_l", [P, 2, NB, XD], F32R)
        pT_h, pT_l = two("pT_h", [P, UH, P], F32R), two("pT_l", [P, UH, P], F32R)
        wo_h, wo_l = two("wo_h", [P, 2, GH, E], F32R), two("wo_l", [P, 2, GH, E], F32R)
        Q = two("Q", [P, GH, NB * P])
        ra = two("ra", [P, 2, HALF_TOK])
        rb = two("rb", [P, 2, HALF_TOK])
        maski = probsT[:].rearrange("p i h q -> p (i h q)").bitcast(I32).rearrange("p (b k) -> p b k", b=NB)
        bias = two("bias", [P, NB, P])
        oT_h, oT_l = two("oT_h", [P, GH, P], F32R), two("oT_l", [P, GH, P], F32R)
        second.close()

        third = ExitStack()

        def three(name, shape, dt=F32):
            return third.enter_context(nc.sbuf_tensor(name, shape, dt))

        xn3 = three("xn3", [P, NB, E])
        xn3T = three("xn3T", [P, EC, NB * P])
        rw = three("rw", [NE, E])
        rwT = three("rwT", [P, EC, NE])
        rb_row = three("rb_row", [P, NE])
        eb = three("eb", [P, E])
        lg = three("lg", [P, NB, NE])
        lmax = three("lmax", [P, NB])
        lsum = three("lsum", [P, NB])
        lrs = three("lrs", [P, NB])
        lsh = three("lsh", [P, NB, NE])
        lex = three("lex", [P, NB, NE])
        lsc = three("lsc", [P, NB, NE])
        top = three("top", [P, NB, TOP])
        cut = three("cut", [P, NB, NE])
        wd = three("wd", [P, NB, NE])
        wsum = three("wsum", [P, NB])
        wdT = three("wdT", [P, NB * P])
        third.close()

        x_in = [sem(f"x_in{b}") for b in range(NB)]
        weight_in = [sem(f"weight_in{k}") for k in range(11)]
        ring_in = [sem(f"ring_in{i}") for i in range(RING)]
        ident_in, small_in, pos_in = sem("ident_in"), sem("small_in"), sem("pos_in")
        wo1_in, context_in, gathered, kv_in = sem("wo1_in"), sem("context_in"), sem("gathered"), sem("kv_in")
        weight_h, weight_l, pool_weight_l = sem("weight_h"), sem("weight_l"), sem("pool_weight_l")
        ring_h, ring_l = sem("ring_h"), sem("ring_l")
        mask_in, ffn_in, stored, kv_stored = sem("mask_in"), sem("ffn_in"), sem("stored"), sem("kv_stored")
        eps_set, stats_done, aggr_done, mv_done = sem("eps_set"), sem("stats_done"), sem("aggr_done"), sem("mv_done")
        spread_done, rstd_done = sem("spread_done"), sem("rstd_done")
        pos_a, pos_b, pos_ready = sem("pos_a"), sem("pos_b"), sem("pos_ready")
        vz_zero, rest_zero = sem("vz_zero"), sem("rest_zero")
        xn_ready, xnT_ps, xnT_hs, xnT_ls = sem("xn_ready"), sem("xnT_ps"), sem("xnT_hs"), sem("xnT_ls")
        cxT_ps, cxT_hs, cxT_ls = sem("cxT_ps"), sem("cxT_hs"), sem("cxT_ls")
        q_ps, kv_ps, kx_ps, vx_ps = sem("q_ps"), sem("kv_ps"), sem("kx_ps"), sem("vx_ps")
        qab_done, qr_ready, kab_done, kr_ready = sem("qab_done"), sem("qr_ready"), sem("kab_done"), sem("kr_ready")
        v_taken, v_ready, kxab_done = sem("v_taken"), sem("v_ready"), sem("kxab_done")
        kxr_ready, vx_ready = sem("kxr_ready"), sem("vx_ready")
        qT_ps, qT_hs, qT_ls, kT_ps, kT_hs, kT_ls = (sem(n) for n in ("qT_ps", "qT_hs", "qT_ls", "kT_ps", "kT_hs",
                                                                     "kT_ls"))
        kTz_hs, kTz_ls = sem("kTz_hs"), sem("kTz_ls")
        kxT_ps, kxT_ready = sem("kxT_ps"), sem("kxT_ready")
        at_ready, o_ps, x1_ready = sem("at_ready"), sem("o_ps"), sem("x1_ready")
        s_ready, masked, exp_done, rsum_ready = sem("s_ready"), sem("masked"), sem("exp_done"), sem("rsum_ready")
        v_hs, v_ls, pT_ls = sem("v_hs"), sem("v_ls"), sem("pT_ls")
        prob_ready, pT_ps, pT_ready, av_done = sem("prob_ready"), sem("pT_ps"), sem("pT_ready"), sem("av_done")
        xn2_ready, xn2T_ps, xn2T_hs, xn2T_ls = sem("xn2_ready"), sem("xn2T_ps"), sem("xn2T_hs"), sem("xn2T_ls")
        tab_ps, tab_ready, bias_ready = sem("tab_ps"), sem("tab_ready"), sem("bias_ready")
        qp_done, rope_ab, q_ready = sem("qp_done"), sem("rope_ab"), sem("q_ready")
        oT_hs, oT_ls, y_done, acc_done = sem("oT_hs"), sem("oT_ls"), sem("y_done"), sem("acc_done")
        xn3_ready, xn3T_ps, xn3T_ready = sem("xn3_ready"), sem("xn3T_ps"), sem("xn3T_ready")
        rwT_ps, rwT_ready, lg_ps, ffn_step = sem("rwT_ps"), sem("rwT_ready"), sem("lg_ps"), sem("ffn_step")
        lsh_ready, wd_ready = sem("lsh_ready"), sem("wd_ready")
        lex_done, wdT_ps, wdT_ready = sem("lex_done"), sem("wdT_ps"), sem("wdT_ready")
        mix_ps, fin_ready = sem("mix_ps"), sem("fin_ready")

        ONE, STORE_ONE = 1, 16
        sp_passed, dve_passed = sem("sp_passed"), sem("dve_passed")

        HALVES = [(half, slice(half * UH // 2, (half + 1) * UH // 2)) for half in range(2)]

        CROSS0 = NB * NU
        PIECES = [(half, head) for half in range(2) for head in range(GH)]
        LEAD = 7
        TURN_ROW = {2: 0, 3: 1, 4: 2, 5: 3, 6: 4, 7: 5}
        TURN_BANK = [7, 7, 7, 7, 7, 6, 5, 6]
        TABLE_ROWS = {2: (0, 2), 3: (2, 4), 4: (4, 6), 6: (6, 8)}
        BATCHES = [(0, 3), (3, 6), (6, 8)]
        MIX_BANK = [2, 3, 6, 2, 3, 6, 7, 0]

        def piece_at(slot):
            n = slot + LEAD
            return (0, n) if n < 8 else (1, n - 8)

        def row(t, b):
            return t[:, bass.ds(b, 1), :].rearrange("p o n -> p (o n)")

        def as_read(t):
            return t.bitcast(F32)

        wq_d, wk_d, wv_d, wk2_d, wv2_d = (w.rearrange("(c p) n -> p c n", p=P) for w in (wq_s, wk_s, wv_s, wk_x, wv_x))
        weights1 = [(wq1_h[:, 2 * c:2 * c + 2, :], wq1_l[:, 2 * c:2 * c + 2, :], [wq_d[:, 2 * c:2 * c + 2, :]], 2)
                    for c in range(EC // 2)]
        weights1 += [(wkv1_h[:], wkv1_l[:], [wk_d, wv_d], EC)]
        weights1 += [(h[:, c:c + 1, :], l[:, c:c + 1, :], [d[:, c:c + 1, :]], 1)
                     for h, l, d in ((wk2_h, wk2_l, wk2_d), (wv2_h, wv2_l, wv2_d)) for c in range(EC)]
        SELF_W, KEY_W, VALUE_W = 3, 7, 11
        POOL_W = (3, 5, 7)
        places = [ring[:, 0:2, :], ring[:, 2:4, :], vx[:].rearrange("p (i n) -> p i n", i=2), kxT[:], kxr[:],
                  wo1[:, 0:2, :], wo1[:, 2:4, :]]

        def wait_for_split(engine, n):
            by_pool = len([k for k in POOL_W if k < n])
            engine.wait_ge(weight_l, n - by_pool)
            if by_pool:
                engine.wait_ge(pool_weight_l, by_pool)

        def loaded(k):
            return places[k % len(places)].rearrange("p i n -> p (i n)").rearrange("p (c n) -> p c n",
                                                                                   c=weights1[k][3])

        block = whole.enter_context(nc.Block())

        @block.sync
        def _(sp):
            sp.sem_inc(kv_stored, STORE_ONE)
            sp.dma_start(ident[:], c_ident).then_inc(ident_in, 16)
            sp.dma_start(X[:, 0, :], x[0]).then_inc(x_in[0], 16)
            sp.dma_start(cx[:], ctx[0]).then_inc(context_in, 16)
            for k, (_, _, sources, blocks) in enumerate(weights1):
                if k == SELF_W:
                    for b in range(1, NB):
                        sp.dma_start(X[:, b, :], x[b]).then_inc(x_in[b], 16)
                if k >= len(places):
                    wait_for_split(sp, k - len(places) + 1)
                width = 2 * E // blocks // len(sources)
                for q, source in enumerate(sources):
                    sp.dma_start(loaded(k)[:, :, q * width:(q + 1) * width], source).then_inc(weight_in[k], 16)
            wait_for_split(sp, len(places))
            for g in range(NG):
                sp.dma_start(wo1[SD * g:SD * (g + 1), :, :],
                             wo_s[g * GH * SD:(g + 1) * GH * SD, :].rearrange("(j d) n -> d j n", d=SD))\
                    .then_inc(wo1_in, 16)

            wait_for_split(sp, len(places) + 2)

            def cross_weights(g, u):
                if u < GH:
                    source = wq_x[:, bass.ds(g * (GH * XD) + u * XD, XD)].rearrange("(c p) n -> p c n", p=P)
                    to = ring[:, u % RING, :].rearrange("p (c n) -> p c n", c=EC)
                else:
                    source = wo_x[bass.ds(g * (GH * XD) + (u - GH) * XD, XD), :]
                    to = ring[:, u % RING, :]
                sp.dma_start(to, source).then_inc(ring_in[u % RING], 16)

            for u in range(RING):
                cross_weights(0, u)

            def row_stores(r, last):
                if not last:
                    sp.wait_ge(cxT_ps, ONE + r + 1)
                    sp.sem_inc(sp_passed)
                    sp.dma_start(cx[:], ctx[bass.ds(r + 1, 1)].rearrange("o p n -> p (o n)")).then_inc(context_in, 16)
                sp.wait_ge(kxT_ready, ONE + 2 * r + 2)
                sp.sem_inc(sp_passed)
                sp.dma_start(k_dram[:, :, bass.ds(r * P, P)].rearrange("g d t -> d g t"), kxT[:])\
                    .then_inc(kv_stored, 16)
                sp.wait_ge(vx_ready, ONE + 2 * r + 2)
                sp.sem_inc(sp_passed)
                sp.dma_start(v_dram[bass.ds(r, 1)].rearrange("o p n -> p (o n)"), vx[:]).then_inc(kv_stored, 16)

            with sp.Fori(0, NB - 1) as r:
                row_stores(r, False)
            row_stores(NB - 1, True)
            sp.wait_ge(x1_ready, ONE + NB)
            sp.wait_ge(kv_stored, STORE_ONE + 32 * NB)
            sp.dma_start(maski, mask.rearrange("b q k -> q b k")).then_inc(mask_in, 16)
            sp.dma_start(k_g[:, 0, :], k_dram[0]).then_inc(kv_in, 16)
            sp.dma_start(v_in[:], v_dram[:, :, 0:XD].rearrange("b k d -> k b d")).then_inc(kv_in, 16)
            for k in range(RING, 8 + RING):
                sp.wait_ge(ring_l, ONE + k - RING + 1)
                cross_weights(k // 8, k % 8)

            def next_group(g, i, last):
                sp.wait_ge(s_ready, ONE + CROSS0 + g * NU)
                sp.sem_inc(sp_passed)
                sp.wait_ge(v_ls, ONE + g + 1)
                sp.sem_inc(sp_passed)
                sp.dma_start(k_g[:, 1 - i, :], k_dram[bass.ds(g + 1, 1)].rearrange("o d t -> d (o t)"))\
                    .then_inc(kv_in, 16)
                sp.dma_start(v_in[:], v_dram[:, :, bass.ds((g + 1) * XD, XD)].rearrange("b k d -> k b d"))\
                    .then_inc(kv_in, 16)
                for k in range(RING, 8 if last else 8 + RING):
                    sp.wait_ge(ring_l, ONE + (g + 1) * 8 + k - RING + 1)
                    sp.sem_inc(sp_passed)
                    cross_weights(g + 1 + k // 8, k % 8)

            with sp.Fori(0, NG // 2 - 1) as g2:
                for i in range(2):
                    next_group(g2 * 2 + i, i, False)
            next_group(NG - 2, 0, True)
            sp.wait_ge(qp_done, ONE + NG * 8)
            sp.wait_ge(rope_ab, ONE + NG * 8)
            sp.dma_start(rw[:], router_w).then_inc(ffn_in, 16)
            sp.dma_start(eb[0:NE, :], expert_b).then_inc(ffn_in, 16)
            sp.dma_start(rb_row[:], router_b.rearrange("(o n) -> o n", o=1).to_broadcast([P, NE]))\
                .then_inc(ffn_in, 16)
            for b in range(NB):
                sp.wait_ge(fin_ready, b + 1)
                sp.dma_start(out[b], X[:, b, :]).then_inc(stored, 16)
            sp.wait_ge(stored, 16 * NB)

        @block.gpsimd
        def _(pool):
            for started in (qr_ready, kxr_ready, kTz_hs, prob_ready, q_ready, ring_l):
                pool.sem_inc(started, ONE)
            pool.dma_start(posi[:], pos).then_inc(pos_in, 16)
            pool.dma_start(rope_s[:], c_rope_self).then_inc(small_in, 16)
            pool.dma_start(rows[:], c_rows).then_inc(small_in, 16)
            pool.dma_start(causal[:], c_causal).then_inc(small_in, 16)
            nc.gpsimd.memset(vz[:], 0.0).then_inc(vz_zero, 1)
            pool.wait_ge(pos_ready, 1)
            for b in range(NB):
                pool.indirect_dma_start(out=rope_x[:, b, :], out_offset=None, in_=c_rope_cross,
                                        in_offset=bass.IndirectOffsetOnAxis(ap=posu[:, b:b + 1], axis=0))\
                    .then_inc(gathered, 16)

            def normalise(i, n, read):
                pool.wait_ge(pT_ps, ONE + read)
                for half, h in HALVES:
                    pool.wait_ge(rsum_ready, ONE + 2 * n + half + 1)
                    nc.gpsimd.tensor_tensor(probs[:, i, h], exps[:, i, h],
                                            rsums[:, i, h].unsqueeze(2).to_broadcast([P, UH // 2, P]), ALU.mult)\
                        .then_inc(prob_ready, 1)

            def query_sum(r):
                pool.wait_ge(qab_done, ONE + r + 1)
                pool.wait_ge(qT_ps, ONE + r)
                by_group = "p (g j d) -> p g j d"
                nc.gpsimd.tensor_tensor(qr[:].rearrange("p (j g d) -> p g j d", j=GH, g=NG),
                                        qa[:].rearrange(by_group, g=NG, j=GH), qb[:].rearrange(by_group, g=NG, j=GH),
                                        ALU.add).then_inc(qr_ready, 1)

            def spread_keys_high(r):
                pool.wait_ge(kT_hs, ONE + r + 1)
                pool.wait_ge(s_ready, ONE + r * NU)
                nc.gpsimd.tensor_tensor(kTz_h[:], as_read(kT_h[:]).unsqueeze(1).to_broadcast([P, NG, P]),
                                        rows[:].unsqueeze(2).to_broadcast([P, NG, P]), ALU.mult).then_inc(kTz_hs, 1)

            def cross_key_sum(r, i):
                pool.wait_ge(kxab_done, ONE + 2 * r + i + 1)
                pool.wait_ge(kxT_ps, ONE + 2 * r)
                nc.gpsimd.tensor_tensor(kxr[:, i], kxa[:], kxb[:], ALU.add).then_inc(kxr_ready, 1)

            def self_slot(r, u, last):
                n = r * NU + u
                if u == 6 and not last:
                    spread_keys_high(r + 1)
                if not last or u + 1 < NU:
                    normalise((u + 1) % 2, n + 1, n)
                if u < 2:
                    cross_key_sum(r, u)
                if u == 2 and not last:
                    query_sum(r + 1)

            def split_pool(ks):
                for k in ks:
                    pool.wait_ge(weight_h, k + 1)
                    high, part = weights1[k][0:2]
                    nc.gpsimd.tensor_tensor(part, loaded(k), as_read(high), ALU.subtract).then_inc(pool_weight_l, 1)

            pool.wait_ge(small_in, 48)
            query_sum(0)
            spread_keys_high(0)
            split_pool(POOL_W[0:2])
            normalise(0, 0, 0)
            split_pool(POOL_W[2:3])
            self_slot(0, 0, False)
            with pool.Fori(0, NB - 1) as r:
                for u in range(1, NU):
                    self_slot(r, u, False)
                self_slot(r + 1, 0, False)
            def split_low(g, i, u):
                piece = ring[:, u % RING, :]
                pool.wait_ge(ring_h, ONE + g * 8 + u + 1)
                if u < GH:
                    to, high = wq_l[:, u].rearrange("p c n -> p (c n)"), wq_h[:, u].rearrange("p c n -> p (c n)")
                else:
                    to, high = wo_l[:, i, u - GH, :], wo_h[:, i, u - GH, :]
                nc.gpsimd.tensor_tensor(to, piece, as_read(high), ALU.subtract).then_inc(ring_l, 1)

            for u in range(1, NU):
                self_slot(NB - 1, u, True)
                if u in (3, 4, 5, 6):
                    split_low(0, 0, u - 3)

            pool.wait_ge(x1_ready, ONE + NB)

            def rotary_sum(m, half, head, i):
                pool.wait_ge(rope_ab, ONE + m + 1)
                nc.gpsimd.tensor_tensor(Q[:, head, half * HALF_TOK:(half + 1) * HALF_TOK], ra[:, i], rb[:, i],
                                        ALU.add).then_inc(q_ready, 1)

            for m in range(LEAD):
                rotary_sum(m, *PIECES[m], m % 2)
                if m in (4, 5):
                    normalise(m - 4, CROSS0 + m - 4, CROSS0 + m - 5)
                if m >= 3:
                    split_low(0, 0, GH + m - 3)

            def group(g, i, last):
                for b in range(NB):
                    n = CROSS0 + g * NU + b
                    if not last:
                        split_low(g + 1, 1 - i, b)
                    if b + 2 < NB or not last:
                        normalise(b % 2, n + 2, n + 1)
                    ahead, k = piece_at(b)
                    if not (ahead and last):
                        half, head = PIECES[k]
                        pool.wait_ge(s_ready, ONE + CROSS0 + (g + ahead - 1) * NU + half * 4 + 4)
                        rotary_sum(g * 8 + LEAD + b, half, head, (LEAD + b) % 2)
                    if last and b == 2:
                        pool.wait_ge(qp_done, ONE + NG * 8)
                        pool.wait_ge(rope_ab, ONE + NG * 8)
                        pool.wait_ge(prob_ready, ONE + 2 * (n + 3))
                        nc.gpsimd.memset(wdT[NE:P, :], 0.0).then_inc(rest_zero, 1)
                        pool.wait_ge(rest_zero, 1)
                        nc.gpsimd.memset(eb[NE:P, :], 0.0).then_inc(rest_zero, 1)
                        pool.wait_ge(rest_zero, 2)

            with pool.Fori(0, NG // 2 - 1) as g2:
                for i in range(2):
                    group(g2 * 2 + i, i, False)
            group(NG - 2, 0, False)
            group(NG - 1, 1, True)

        @block.scalar
        def _(act):
            for started in (v_hs, xnT_hs, cxT_hs, v_taken, v_ready, vx_ready, qT_hs, kT_hs, kxT_ready, exp_done, pT_ready,
                            at_ready, oT_hs, ring_h):
                act.sem_inc(started, ONE)

            def spread_of(first_row, end_row, measured):
                act.wait_ge(mv_done, measured)
                nc.scalar.activation(spread[:, first_row:end_row], mean_var[:, first_row:end_row, 1], ACT.Sqrt,
                                     bias=eps[:, 0:1]).then_inc(spread_done, 1)

            loads = [0]

            def load_table(function):
                n = loads[0]
                loads[0] += 1
                nc.scalar.activation(unused[:, n:n + 1], eps[:], function)

            def exponentials(i, n, used):
                act.wait_ge(prob_ready, ONE + 2 * used)
                for half, heads in HALVES:
                    act.wait_ge(masked, ONE + 2 * n + half + 1)
                    for h in range(heads.start, heads.stop):
                        last = nc.scalar.activation(exps[:, i, h, :], neg_scores[:, i, h, :], ACT.Exp,
                                                    bias=neg_max[:, i, h:h + 1], scale=-1.0,
                                                    accum_out=sums[:, i, h:h + 1])
                    last.then_inc(exp_done, 1)

            def take_probsT(i, n, used, ps):
                act.wait_ge(pT_ps, ONE + n + 1)
                act.wait_ge(av_done, ONE + used)
                nc.scalar.copy(probsT[:, i], ps[:].rearrange("p (h q) -> p h q", h=UH)).then_inc(pT_ready, 1)

            def split_high1(ks):
                for k in ks:
                    act.wait_ge(weight_in[k], 16 * len(weights1[k][2]))
                    nc.scalar.copy(weights1[k][0], loaded(k)).then_inc(weight_h, 1)

            def take_xnT(r):
                act.wait_ge(xnT_ps, ONE + r + 1)
                act.wait_ge(kv_ps, ONE + r)
                nc.scalar.copy(xnT_h[:], bank[7][:].rearrange("p (c t) -> p c t", c=EC)).then_inc(xnT_hs, 1)

            def take_v(r):
                act.wait_ge(kv_ps, ONE + r + 1)
                act.wait_ge(kab_done, ONE + r + 1)
                act.wait_ge(v_ready, ONE + r)
                nc.scalar.copy(vs[:], bank[6][:, P:2 * P]).then_inc(v_taken, 1)

            def place_v(r):
                act.wait_ge(v_taken, ONE + r + 1)
                act.wait_ge(av_done, ONE + r * NU)
                nc.scalar.copy(vz[:].rearrange("p (g c) -> p g c", c=VZ)[:, :, 0:SD],
                               vs[:].rearrange("p (g d) -> p g d", d=SD)).then_inc(v_ready, 1)

            def take_kT(r):
                act.wait_ge(kT_ps, ONE + r + 1)
                act.wait_ge(kTz_hs, ONE + r)
                nc.scalar.copy(kT_h[:], bank[6][:, 0:P]).then_inc(kT_hs, 1)

            def take_qT(r):
                act.wait_ge(qT_ps, ONE + r + 1)
                act.wait_ge(s_ready, ONE + r * NU)
                nc.scalar.copy(qT_h[:], bank[7][:].rearrange("p (j t) -> p j t", j=GH)).then_inc(qT_hs, 1)

            def take_cxT(r):
                act.wait_ge(cxT_ps, ONE + r + 1)
                act.wait_ge(vx_ps, ONE + 2 * r)
                nc.scalar.copy(cxT_h[:], bank[5][:].rearrange("p (c t) -> p c t", c=EC)).then_inc(cxT_hs, 1)

            def take_kxT(r, i):
                act.wait_ge(kxT_ps, ONE + 2 * r + i + 1)
                wait_for_split(act, VALUE_W)
                act.wait_ge(kv_stored, STORE_ONE + 32 * r)
                nc.scalar.copy(kxT[:, 4 * i:4 * i + 4, :], bank[5 + i][:].rearrange("p (g t) -> p g t", g=4))\
                    .then_inc(kxT_ready, 1)

            def take_vx(r, i):
                act.wait_ge(vx_ps, ONE + 2 * r + i + 1)
                nc.scalar.copy(vx[:, i * 512:(i + 1) * 512], bank[5][:]).then_inc(vx_ready, 1)

            def take_attention(r):
                act.wait_ge(av_done, ONE + r * NU + NU)
                act.wait_ge(o_ps, ONE + r)
                nc.scalar.copy(atT[:], bank[4][:].rearrange("p (j t) -> p j t", j=GH)).then_inc(at_ready, 1)

            def self_slot(r, u, last):
                n = r * NU + u
                take_probsT(u % 2, n, r * NU + max(u - 1, 0), bank[2 + u % 2])
                if u == 6 and not last:
                    take_qT(r + 1)
                if u == 7:
                    take_attention(r)
                if not last or u + 1 < NU:
                    exponentials((u + 1) % 2, n + 1, n)
                if u == 1 and not last:
                    take_xnT(r + 1)
                if u == 3:
                    if not last:
                        take_v(r + 1)
                    take_kxT(r, 0)
                if u == 4:
                    if not last:
                        take_kT(r + 1)
                    take_vx(r, 0)
                if u == 5:
                    take_kxT(r, 1)
                if u == 6:
                    take_vx(r, 1)
                if u == 7 and not last:
                    place_v(r + 1)
                    take_cxT(r + 1)

            act.wait_ge(eps_set, 1)
            load_table(ACT.Sqrt)
            spread_of(0, 1, 1)
            take_cxT(0)
            split_high1(range(0, 2))
            take_xnT(0)
            split_high1(range(2, 5))
            take_v(0)
            take_kT(0)
            spread_of(1, NB, NB)
            load_table(ACT.Exp)
            take_qT(0)
            act.wait_ge(vz_zero, 1)
            place_v(0)
            split_high1(range(5, 7))
            exponentials(0, 0, 0)
            split_high1(range(7, 9))
            self_slot(0, 0, False)
            split_high1(range(9, 11))
            with act.Fori(0, NB - 1) as r:
                for u in range(1, NU):
                    self_slot(r, u, False)
                self_slot(r + 1, 0, False)
            def split_high(g, i, u, first_group=False):
                piece = ring[:, u % RING, :]
                act.wait_ge(ring_in[u % RING], 32 * g + 16 * (u // RING + 1))
                if u < GH:
                    to = wq_h[:, u].rearrange("p c n -> p (c n)")
                    if not first_group:
                        act.wait_ge(qp_done, ONE + g * 8 - 8 + 5 + u)
                else:
                    to = wo_h[:, i, u - GH, :]
                    if not first_group:
                        act.wait_ge(y_done, ONE + g * NU - NU)
                nc.scalar.copy(to, piece).then_inc(ring_h, 1)

            def values_high(g, i):
                act.wait_ge(kv_in, 32 * (g + 1))
                nc.scalar.copy(v_h[:, i], v_in[:]).then_inc(v_hs, 1)

            def take_xn2T(b):
                act.wait_ge(xn2T_ps, b + 1)
                nc.scalar.copy(xn2T_h[:, :, b * P:(b + 1) * P],
                               bank[TURN_BANK[b]][:].rearrange("p (c t) -> p c t", c=EC)).then_inc(xn2T_hs, 1)

            for u in range(1, NU):
                self_slot(NB - 1, u, True)
                if u == 1:
                    load_table(ACT.Sqrt)
                    spread_of(0, NB - 1, 2 * NB - 1)
                    load_table(ACT.Exp)
                    act.wait_ge(kv_ps, ONE + NB)
                    act.wait_ge(kx_ps, ONE + 2 * NB)
                if u in TURN_ROW:
                    take_xn2T(TURN_ROW[u])
                if u in TABLE_ROWS:
                    a, z = TABLE_ROWS[u]
                    act.wait_ge(tab_ps, z // 2)
                    nc.scalar.copy(table[:, :, a * P:z * P], bank[6][:].rearrange("p (i t) -> p i t", i=2))\
                        .then_inc(tab_ready, 1)
                if u in (3, 4, 5, 6):
                    split_high(0, 0, u - 3, True)
            take_xn2T(6)
            load_table(ACT.Sqrt)
            spread_of(NB - 1, NB, 2 * NB)
            load_table(ACT.Exp)
            act.wait_ge(x1_ready, ONE + NB)
            act.wait_ge(kv_stored, STORE_ONE + 32 * NB)
            for u in range(GH, GH + 2):
                split_high(0, 0, u, True)
            take_xn2T(NB - 1)
            values_high(0, 0)
            for u in range(GH + 2, 8):
                split_high(0, 0, u, True)
            for u in range(2):
                exponentials(u, CROSS0 + u, CROSS0 + u - 1)

            def copy_rows(k):
                for b in range(*BATCHES[k]):
                    act.wait_ge(xn3T_ps, b + 1)
                    nc.scalar.copy(xn3T[:, :, b * P:(b + 1) * P],
                                   bank[b % 2][:].rearrange("p (c t) -> p c t", c=EC)).then_inc(xn3T_ready, 1)

            def router_exponentials(k):
                a, z = BATCHES[k]
                act.wait_ge(lsh_ready, k + 1)
                nc.scalar.activation(lex[:, a:z, :], lsh[:, a:z, :], ACT.Exp).then_inc(lex_done, 1)

            def copy_weights(k):
                a, z = BATCHES[k]
                act.wait_ge(wdT_ps, k + 1)
                nc.scalar.copy(wdT[0:NE, a * P:z * P], bank[4][0:NE, 0:(z - a) * P]).then_inc(wdT_ready, 1)

            def group(g, i, last):
                for b in range(NB):
                    n = CROSS0 + g * NU + b
                    act.wait_ge(pT_ps, ONE + n + 1)
                    act.wait_ge(av_done, ONE + n)
                    nc.scalar.copy(pT_h[:], bank[4][:].rearrange("p (h q) -> p h q", h=UH)).then_inc(pT_ready, 1)
                    act.wait_ge(av_done, ONE + n + 1)
                    act.wait_ge(y_done, ONE + g * NU + b)
                    nc.scalar.copy(oT_h[:], bank[6][:].rearrange("p (h q) -> p h q", h=GH)).then_inc(oT_hs, 1)
                    if last and b == 4:
                        copy_rows(0)
                    if b + 2 < NB or not last:
                        exponentials(b % 2, n + 2, n + 1)
                    if not last:
                        split_high(g + 1, 1 - i, b)
                        if b == 3:
                            act.wait_ge(av_done, ONE + CROSS0 + g * NU)
                            values_high(g + 1, 1 - i)
                        continue
                    if b == 2:
                        act.wait_ge(rwT_ps, 1)
                        nc.scalar.copy(rwT[:], bank[5][:, 0:EC * NE].rearrange("p (c n) -> p c n", c=EC))\
                            .then_inc(rwT_ready, 1)
                    if b in (3, 6):
                        spread_of(*BATCHES[b // 3 - 1], 2 * NB + b)
                        load_table(ACT.Exp)
                    if b == 5:
                        router_exponentials(0)
                    if b == 7:
                        copy_rows(1)
                        router_exponentials(1)
                        copy_weights(0)

            with act.Fori(0, NG // 2 - 1) as g2:
                for i in range(2):
                    group(g2 * 2 + i, i, False)
            group(NG - 2, 0, False)
            group(NG - 1, 1, True)
            load_table(ACT.Sqrt)
            spread_of(*BATCHES[2], 3 * NB)
            load_table(ACT.Exp)
            copy_rows(2)
            copy_weights(1)
            router_exponentials(2)
            copy_weights(2)

        @block.vector
        def _(dve):
            for started in (v_ls, pT_ls, xn_ready, xnT_ls, cxT_ls, qab_done, kab_done, kr_ready, kxab_done, kT_ls,
                            kTz_ls, qT_ls,
                            masked, rsum_ready, x1_ready, rope_ab, oT_ls, acc_done):
                dve.sem_inc(started, ONE)
            nc.vector.memset(eps[:], EPS).then_inc(eps_set, 1)

            def statistics(b, n):
                nc.vector.bn_stats(stats[:, 0, :], row(X, b)).then_inc(stats_done, 1)
                dve.wait_ge(stats_done, n + 1)
                dve.sem_inc(dve_passed)
                nc.vector.bn_aggr(one_row[:], stats[:, 0, :]).then_inc(aggr_done, 1)
                dve.wait_ge(aggr_done, n - NB + 1)
                dve.sem_inc(dve_passed)
                nc.vector.tensor_copy(row(mean_var, b), one_row[:]).then_inc(mv_done, 1)
                dve.wait_ge(mv_done, n + 1)

            def invert_spread(n, first_row=0, end_row=NB):
                dve.wait_ge(spread_done, n + 1)
                nc.vector.reciprocal(rstd[:, first_row:end_row], spread[:, first_row:end_row]).then_inc(rstd_done, 1)
                dve.wait_ge(rstd_done, n + 1)

            def normed(to, b):
                return nc.vector.tensor_scalar(to, row(X, b), row(mean_var, b)[:, 0:1], rstd[:, bass.ds(b, 1)],
                                               ALU.subtract, ALU.mult)

            def mask_scores(i, n, used, ps, added, scale):
                dve.wait_ge(s_ready, ONE + n + 1)
                dve.wait_ge(exp_done, ONE + 2 * used)
                dve.sem_inc(dve_passed)
                for half, heads in HALVES:
                    for h in range(heads.start, heads.stop):
                        last = nc.vector.tensor_tensor_reduce(
                            out=neg_scores[:, i, h, :], in0=ps[:, h * P:(h + 1) * P], in1=added, scale=-scale,
                            scalar=BIG, op0=ALU.add, op1=ALU.min, accum_out=neg_max[:, i, h:h + 1])
                    last.then_inc(masked, 1)

            def invert_sums(i, n):
                for half, h in HALVES:
                    dve.wait_ge(exp_done, ONE + 2 * n + half + 1)
                    nc.vector.reciprocal(rsums[:, i, h], sums[:, i, h]).then_inc(rsum_ready, 1)

            def rotate(to_a, to_b, src, heads, width, cos, sin_low, sin_high):
                half = width // 2
                v, a, b_ = (t.rearrange("p (h d) -> p h d", d=width) for t in (src, to_a, to_b))
                nc.vector.tensor_tensor(a, v, cos.unsqueeze(1).to_broadcast([P, heads, width]), ALU.mult)
                nc.vector.tensor_tensor(b_[:, :, 0:half], v[:, :, half:width],
                                        sin_low.unsqueeze(1).to_broadcast([P, heads, half]), ALU.mult)
                return nc.vector.tensor_tensor(b_[:, :, half:width], v[:, :, 0:half],
                                               sin_high.unsqueeze(1).to_broadcast([P, heads, half]), ALU.mult)

            def low(to, ps, high):
                return nc.vector.tensor_tensor(to, ps, as_read(high), ALU.subtract)

            def split_low1(ks):
                for k in ks:
                    if k in POOL_W:
                        continue
                    dve.wait_ge(weight_h, k + 1)
                    high, part = weights1[k][0:2]
                    low(part, loaded(k), high).then_inc(weight_l, 1)

            def norm_row(r):
                dve.wait_ge(xnT_ps, ONE + r)
                normed(xn[:], r).then_inc(xn_ready, 1)

            def low_xnT(r):
                dve.wait_ge(xnT_hs, ONE + r + 1)
                low(xnT_l[:], bank[7][:].rearrange("p (c t) -> p c t", c=EC), xnT_h[:]).then_inc(xnT_ls, 1)

            def low_cxT(r):
                dve.wait_ge(cxT_hs, ONE + r + 1)
                low(cxT_l[:], bank[5][:].rearrange("p (c t) -> p c t", c=EC), cxT_h[:]).then_inc(cxT_ls, 1)

            def rotate_q(r):
                dve.wait_ge(q_ps, ONE + r + 1)
                dve.wait_ge(qr_ready, ONE + r)
                rotate(qa[:], qb[:], bank[7][:], E // SD, SD, rope_s[:, 0:SD], rope_s[:, SD:SD + 8],
                       rope_s[:, SD + 8:2 * SD]).then_inc(qab_done, 1)

            def rotate_k(r):
                dve.wait_ge(kv_ps, ONE + r + 1)
                dve.wait_ge(kr_ready, ONE + r)
                rotate(ka[:], kb[:], bank[6][:, 0:P], NG, SD, rope_s[:, 0:SD], rope_s[:, SD:SD + 8],
                       rope_s[:, SD + 8:2 * SD]).then_inc(kab_done, 1)
                dve.wait_ge(kab_done, ONE + r + 1)
                dve.wait_ge(kT_ps, ONE + r)
                nc.vector.tensor_tensor(kr[:], ka[:], kb[:], ALU.add).then_inc(kr_ready, 1)

            def rotate_kx(r, i):
                dve.wait_ge(kx_ps, ONE + 2 * r + i + 1)
                dve.wait_ge(kxr_ready, ONE + 2 * r + i)
                tab = row(rope_x, r)
                rotate(kxa[:], kxb[:], bank[5 + i][:], 4, XD, tab[:, 0:128], tab[:, 192:256], tab[:, 128:192])\
                    .then_inc(kxab_done, 1)

            def low_kT(r):
                dve.wait_ge(kT_hs, ONE + r + 1)
                dve.wait_ge(kTz_ls, ONE + r)
                low(kT_l[:], bank[6][:, 0:P], kT_h[:]).then_inc(kT_ls, 1)

            def spread_keys_low(r):
                dve.wait_ge(kT_ls, ONE + r + 1)
                dve.wait_ge(s_ready, ONE + r * NU)
                nc.vector.tensor_tensor(kTz_l[:], kT_l[:].unsqueeze(1).to_broadcast([P, NG, P]),
                                        rows[:].unsqueeze(2).to_broadcast([P, NG, P]), ALU.mult).then_inc(kTz_ls, 1)

            def low_qT(r):
                dve.wait_ge(qT_hs, ONE + r + 1)
                low(qT_l[:], bank[7][:].rearrange("p (j t) -> p j t", j=GH), qT_h[:]).then_inc(qT_ls, 1)

            def add_attention(r):
                dve.wait_ge(o_ps, ONE + r + 1)
                nc.vector.tensor_tensor(row(X, r), bank[7][:], row(X, r), ALU.add).then_inc(x1_ready, 1)
                dve.wait_ge(x1_ready, ONE + r + 1)
                dve.sem_inc(dve_passed)
                statistics(r, r + NB)

            def self_slot(r, u, last, first=False):
                n = r * NU + u
                if not last or u + 1 < NU:
                    mask_scores((u + 1) % 2, n + 1, n, bank[(u + 1) % 2], causal[:], SELF_SCALE)
                if u == 0 and not first:
                    add_attention(r - 1)
                if u == 1 and not last:
                    norm_row(r + 1)
                if u == 6 and not last:
                    spread_keys_low(r + 1)
                    low_qT(r + 1)
                if not last or u + 1 < NU:
                    invert_sums((u + 1) % 2, n + 1)
                if first:
                    split_low1(range(KEY_W, VALUE_W))
                if u < 2:
                    rotate_kx(r, u)
                if not last:
                    if u == 1:
                        low_xnT(r + 1)
                    if u == 2:
                        rotate_q(r + 1)
                    if u == 3:
                        rotate_k(r + 1)
                    if u == 4:
                        low_kT(r + 1)
                    if u == 7:
                        low_cxT(r + 1)

            dve.wait_ge(pos_in, 16)
            nc.vector.tensor_scalar(posf[:], posi[:], 0.0, float(MAXPOS), ALU.is_lt, ALU.mult).then_inc(pos_a, 1)
            dve.wait_ge(pos_a, 1)
            nc.vector.tensor_tensor(posn[:], posi[:], posf[:], ALU.add).then_inc(pos_b, 1)
            dve.wait_ge(pos_b, 1)
            nc.vector.tensor_scalar(posu[:], posn[:], 0.0, float(MAXPOS - 1), ALU.max, ALU.min).then_inc(pos_ready, 1)
            def first_statistics(rows):
                for b in rows:
                    dve.wait_ge(x_in[b], 16)
                    nc.vector.bn_stats(stats[:, b, :], X[:, b, :]).then_inc(stats_done, 1)
                dve.wait_ge(stats_done, rows[-1] + 1)
                for b in rows:
                    nc.vector.bn_aggr(mean_var[:, b, :], stats[:, b, :]).then_inc(mv_done, 1)
                dve.wait_ge(mv_done, rows[-1] + 1)

            first_statistics(range(0, 1))
            invert_spread(0, 0, 1)
            norm_row(0)
            low_cxT(0)
            split_low1(range(0, 2))
            low_xnT(0)
            split_low1(range(2, 3))
            first_statistics(range(1, NB // 2))
            dve.wait_ge(small_in, 48)
            rotate_q(0)
            rotate_k(0)
            first_statistics(range(NB // 2, NB))
            low_kT(0)
            spread_keys_low(0)
            low_qT(0)
            invert_spread(1, 1, NB)
            split_low1(range(3, 5))
            mask_scores(0, 0, 0, bank[0], causal[:], SELF_SCALE)
            split_low1(range(5, 7))
            invert_sums(0, 0)
            dve.wait_ge(gathered, 16 * NB)
            self_slot(0, 0, False, first=True)
            with dve.Fori(0, NB - 1) as r:
                for u in range(1, NU):
                    self_slot(r, u, False)
                self_slot(r + 1, 0, False)
            def norm2(b):
                if b >= 2:
                    dve.wait_ge(xn2T_ps, b - 1)
                normed(xn2[:, b % 2], b).then_inc(xn2_ready, 1)

            def low_xn2T(b):
                dve.wait_ge(xn2T_hs, b + 1)
                t = slice(b * P, (b + 1) * P)
                low(xn2T_l[:, :, t], bank[TURN_BANK[b]][:].rearrange("p (c t) -> p c t", c=EC), xn2T_h[:, :, t])\
                    .then_inc(xn2T_ls, 1)

            for u in range(1, NU):
                self_slot(NB - 1, u, True)
                if u == 1:
                    dve.wait_ge(qr_ready, ONE + NB)
                    dve.wait_ge(kx_ps, ONE + 2 * NB)
                    invert_spread(2, 0, NB - 1)
                    norm2(0)
                if u in TURN_ROW:
                    norm2(TURN_ROW[u] + 1)
                    low_xn2T(TURN_ROW[u])
            low_xn2T(6)
            add_attention(NB - 1)
            dve.wait_ge(kv_stored, STORE_ONE + 32 * NB)
            dve.wait_ge(tab_ready, NB // 2)

            def rotate_piece(m, half, i, summed):
                dve.wait_ge(qp_done, ONE + m + 1)
                dve.wait_ge(q_ready, ONE + summed)
                t = slice(half * HALF_TOK, (half + 1) * HALF_TOK)
                lo, hi = slice(0, XD // 2), slice(XD // 2, XD)
                nc.vector.tensor_tensor(ra[:, i], bank[i][:], cosT[:, t], ALU.mult)
                nc.vector.tensor_tensor(rb[lo, i], bank[i][hi, :], sinT[hi, t], ALU.mult)
                nc.vector.tensor_tensor(rb[hi, i], bank[i][lo, :], sinT[lo, t], ALU.mult).then_inc(rope_ab, 1)

            def values_low(g, i):
                dve.wait_ge(v_hs, ONE + g + 1)
                low(v_l[:, i], v_in[:], v_h[:, i]).then_inc(v_ls, 1)

            for m in range(LEAD):
                rotate_piece(m, PIECES[m][0], m % 2, max(m - 1, 0))
                if m == 1:
                    invert_spread(3, NB - 1, NB)
                    norm2(NB - 1)
                    low_xn2T(NB - 1)
                if m == 3:
                    values_low(0, 0)
                if m == 0:
                    dve.wait_ge(mask_in, 16)
                    nc.vector.tensor_scalar(bias[:], maski, 0.0, NEG, ALU.is_equal, ALU.mult).then_inc(bias_ready, 1)
                    dve.wait_ge(bias_ready, 1)
                if m in (4, 5):
                    u = m - 4
                    mask_scores(u, CROSS0 + u, CROSS0 + u - 1, bank[2 + u], bias[:, u, :], CROSS_SCALE)
                    invert_sums(u, CROSS0 + u)

            steps = [0]

            def step(ins):
                steps[0] += 1
                ins.then_inc(ffn_step, 1)
                dve.wait_ge(ffn_step, steps[0])

            def norm_rows(k):
                invert_spread(4 + k, *BATCHES[k])
                for b in range(*BATCHES[k]):
                    normed(xn3[:, b, :], b).then_inc(xn3_ready, 1)

            def route_logits(k):
                a, z = BATCHES[k]
                wide = [P, z - a, NE]
                dve.wait_ge(lg_ps, k + 1)
                logit_bank = bank[5][:, a * NE:z * NE].rearrange("p (b n) -> p b n", n=NE)
                step(nc.vector.tensor_tensor(lg[:, a:z], logit_bank,
                                             rb_row[:].unsqueeze(1).to_broadcast(wide), ALU.add))
                step(nc.vector.tensor_reduce(lmax[:, a:z], lg[:, a:z], AX.X, ALU.max))
                nc.vector.tensor_tensor(lsh[:, a:z], lg[:, a:z], lmax[:, a:z].unsqueeze(2).to_broadcast(wide),
                                        ALU.subtract).then_inc(lsh_ready, 1)

            def route_scores(k):
                a, z = BATCHES[k]
                wide = [P, z - a, NE]
                dve.wait_ge(lex_done, k + 1)
                step(nc.vector.tensor_reduce(lsum[:, a:z], lex[:, a:z], AX.X, ALU.add))
                step(nc.vector.reciprocal(lrs[:, a:z], lsum[:, a:z]))
                step(nc.vector.tensor_tensor(lsc[:, a:z], lex[:, a:z], lrs[:, a:z].unsqueeze(2).to_broadcast(wide),
                                             ALU.mult))

            def route_top(k):
                a, z = BATCHES[k]
                for b in range(a, z):
                    last = nc.vector.max(top[:, b, :], lsc[:, b, :])
                step(last)
                for b in range(a, z):
                    last = nc.vector.match_replace(out=cut[:, b, :], in_to_replace=top[:, b, :],
                                                   in_values=lsc[:, b, :], imm_value=-1.0)
                step(last)
                nc.vector.scalar_tensor_tensor(out=wd[:, a:z], in0=cut[:, a:z], scalar=0.0, in1=lsc[:, a:z],
                                               op0=ALU.is_lt, op1=ALU.mult).then_inc(wd_ready, 1)
                dve.wait_ge(wd_ready, k + 1)
                step(nc.vector.tensor_reduce(wsum[:, a:z], wd[:, a:z], AX.X, ALU.add))

            def add_own(k):
                for b in range(*BATCHES[k]):
                    last = nc.vector.scalar_tensor_tensor(out=X[:, b, :], in0=xn3[:, b, :], scalar=wsum[:, b:b + 1],
                                                          in1=X[:, b, :], op0=ALU.mult, op1=ALU.add)
                step(last)

            def finish(k):
                for b in range(*BATCHES[k]):
                    dve.wait_ge(mix_ps, b + 1)
                    if k < 2:
                        nc.vector.tensor_tensor(X[:, b, :], bank[MIX_BANK[b]][:], X[:, b, :], ALU.add)\
                            .then_inc(fin_ready, 1)
                    else:
                        nc.vector.scalar_tensor_tensor(out=X[:, b, :], in0=xn3[:, b, :], scalar=wsum[:, b:b + 1],
                                                       in1=bank[MIX_BANK[b]][:], op0=ALU.mult, op1=ALU.add)\
                            .then_inc(fin_ready, 1)

            def add_output(g, b):
                dve.wait_ge(y_done, ONE + g * NU + b + 1)
                dve.wait_ge(acc_done, ONE + g * NU + b)
                nc.vector.tensor_tensor(X[:, b, :], bank[7][:], X[:, b, :], ALU.add).then_inc(acc_done, 1)

            def last_output(b):
                add_output(NG - 1, b)
                dve.wait_ge(acc_done, ONE + (NG - 1) * NU + b + 1)
                statistics(b, 2 * NB + b)

            def group(g, i, last):
                for b in range(NB):
                    n = CROSS0 + g * NU + b
                    dve.wait_ge(pT_ready, ONE + n + 1)
                    dve.wait_ge(av_done, ONE + n)
                    low(pT_l[:], bank[4][:].rearrange("p (h q) -> p h q", h=UH), pT_h[:]).then_inc(pT_ls, 1)
                    if b + 2 < NB or not last:
                        mask_scores(b % 2, n + 2, n + 1, bank[2 + b % 2], bias[:, (b + 2) % NB, :], CROSS_SCALE)
                    if last and b:
                        last_output(b - 1)
                    dve.wait_ge(oT_hs, ONE + g * NU + b + 1)
                    dve.wait_ge(y_done, ONE + g * NU + b)
                    low(oT_l[:], bank[6][:].rearrange("p (h q) -> p h q", h=GH), oT_h[:]).then_inc(oT_ls, 1)
                    ahead, k = piece_at(b)
                    if not (ahead and last):
                        m = g * 8 + LEAD + b
                        rotate_piece(m, PIECES[k][0], (LEAD + b) % 2, m - 1)
                    if b + 2 < NB or not last:
                        invert_sums(b % 2, n + 2)
                    if b == 3 and not last:
                        values_low(g + 1, 1 - i)
                    if last and b == 3:
                        dve.wait_ge(qp_done, ONE + NG * 8)
                        norm_rows(0)
                    if last and b == 5:
                        dve.wait_ge(ffn_in, 48)
                        route_logits(0)
                        route_scores(0)
                    if last and b == 7:
                        add_own(0)
                    if last and b == 6:
                        route_top(0)
                        norm_rows(1)
                    if last and b == 7:
                        route_logits(1)
                        route_scores(1)
                    if not last:
                        add_output(g, b)

            with dve.Fori(0, NG // 2 - 1) as g2:
                for i in range(2):
                    group(g2 * 2 + i, i, False)
            group(NG - 2, 0, False)
            group(NG - 1, 1, True)

            last_output(NB - 1)
            norm_rows(2)
            route_top(1)
            add_own(1)
            finish(0)
            route_logits(2)
            route_scores(2)
            route_top(2)
            finish(1)
            finish(2)

        @block.tensor
        def _(pe):
            for started in (xnT_ps, cxT_ps, q_ps, kv_ps, kx_ps, vx_ps, qT_ps, kT_ps, kxT_ps, o_ps, s_ready, pT_ps,
                            av_done, qp_done, y_done):
                pe.sem_inc(started, ONE)

            def transpose_chunks(ps, src, n=4):
                for c in range(n):
                    last = nc.tensor.transpose(ps[:, c * P:(c + 1) * P], src[:, c * P:(c + 1) * P], ident[:])
                return last

            def product(ps, lhsT, rhs):
                for c in range(EC):
                    last = nc.tensor.matmul(ps, lhsT(c), rhs(c), start=(c == 0), stop=(c == EC - 1))
                return last

            def product3(ps, terms, first=True, final=True):
                for t, (a_h, a_l, b_h, b_l) in enumerate(terms):
                    nc.tensor.matmul(ps, a_h, b_l, start=(first and t == 0), stop=False)
                    nc.tensor.matmul(ps, a_h, b_h, start=False, stop=False)
                    last = nc.tensor.matmul(ps, a_l, b_h, start=False, stop=(final and t == len(terms) - 1))
                return last

            def transpose_probs(i, n, ps):
                pe.wait_ge(prob_ready, ONE + 2 * n + 2)
                for h in range(UH):
                    last = nc.tensor.transpose(ps[:, h * P:(h + 1) * P], probs[:, i, h, :], ident[:])
                last.then_inc(pT_ps, 1)

            def turn_context(r):
                pe.wait_ge(context_in, 16 * r + 16)
                pe.wait_ge(vx_ready, ONE + 2 * r)
                transpose_chunks(bank[5], cx).then_inc(cxT_ps, 1)

            def turn_x(r, added):
                pe.wait_ge(xn_ready, ONE + r + 1)
                pe.wait_ge(x1_ready, ONE + added)
                transpose_chunks(bank[7], xn).then_inc(xnT_ps, 1)

            def make_q(r):
                pe.wait_ge(xnT_hs, ONE + r + 1)
                pe.wait_ge(xnT_ls, ONE + r + 1)
                product3(bank[7][:], [(xnT_h[:, c, :], xnT_l[:, c, :], wq1_h[:, c, :], wq1_l[:, c, :])
                                      for c in range(EC)]).then_inc(q_ps, 1)

            def make_kv(r):
                pe.wait_ge(kxab_done, ONE + 2 * r)
                product3(bank[6][:, 0:2 * P], [(xnT_h[:, c, :], xnT_l[:, c, :], wkv1_h[:, c, :], wkv1_l[:, c, :])
                                               for c in range(EC)]).then_inc(kv_ps, 1)

            def turn_k(r):
                pe.wait_ge(kr_ready, ONE + r + 1)
                pe.wait_ge(v_taken, ONE + r + 1)
                nc.tensor.transpose(bank[6][:, 0:P], kr[:], ident[:]).then_inc(kT_ps, 1)

            def turn_q(r):
                pe.wait_ge(qr_ready, ONE + r + 1)
                transpose_chunks(bank[7], qr).then_inc(qT_ps, 1)

            def make_kx(r, i):
                if i == 0:
                    pe.wait_ge(cxT_hs, ONE + r + 1)
                    pe.wait_ge(cxT_ls, ONE + r + 1)
                else:
                    pe.wait_ge(kT_ls, ONE + r + 1)
                    pe.wait_ge(kxT_ready, ONE + 2 * r)
                n = slice(i * 512, (i + 1) * 512)
                product3(bank[5 + i][:], [(cxT_h[:, c, :], cxT_l[:, c, :], wk2_h[:, c, n], wk2_l[:, c, n])
                                          for c in range(EC)]).then_inc(kx_ps, 1)

            def make_vx(r, i, part=range(EC)):
                if i == 0:
                    wait_for_split(pe, VALUE_W)
                    pe.wait_ge(kxT_ready, ONE + 2 * r + 1)
                else:
                    pe.wait_ge(vx_ready, ONE + 2 * r + 1)
                n = slice(i * 512, (i + 1) * 512)
                last = product3(bank[5][:], [(cxT_h[:, c, :], cxT_l[:, c, :], wv2_h[:, c, n], wv2_l[:, c, n])
                                             for c in part], first=(part[0] == 0), final=(part[-1] == EC - 1))
                if part[-1] == EC - 1:
                    last.then_inc(vx_ps, 1)

            def turn_kx(r, i):
                pe.wait_ge(kxr_ready, ONE + 2 * r + i + 1)
                transpose_chunks(bank[5 + i], kxr[:, i]).then_inc(kxT_ps, 1)

            def scores(u):
                j, g = u // 2, slice(4 * (u % 2), 4 * (u % 2) + 4)
                product3(bank[u % 2][:], [(qT_h[:, j, :], qT_l[:, j, :], kTz_h[:, g, :], kTz_l[:, g, :])])\
                    .then_inc(s_ready, 1)

            def wait_for_row(r):
                for ready in (qT_hs, qT_ls, kTz_hs, kTz_ls):
                    pe.wait_ge(ready, ONE + r + 1)

            def self_slot(r, u, last, fill=None):
                n = r * NU + u
                pe.wait_ge(pT_ready, ONE + r * NU + max(u - 1, 0))
                transpose_probs(u % 2, n, bank[2 + u % 2])
                if u == 0:
                    make_kx(r, 0)
                if u == 1:
                    make_kx(r, 1)
                    if not last:
                        turn_x(r + 1, r)
                if u == 2 and not last:
                    make_q(r + 1)
                if u == 3:
                    if not last:
                        make_kv(r + 1)
                    turn_kx(r, 0)
                if u == 4:
                    if not last:
                        turn_k(r + 1)
                    make_vx(r, 0)
                if u == 5:
                    if not last:
                        pe.wait_ge(kT_ls, ONE + r + 2)
                    else:
                        pe.wait_ge(tab_ready, 3)
                    turn_kx(r, 1)
                    if not last:
                        turn_q(r + 1)
                if u == 5:
                    make_vx(r, 1, range(0, 1))
                if u == 6:
                    make_vx(r, 1, range(1, EC))
                if u == 7 and not last:
                    turn_context(r + 1)
                if fill:
                    fill(u)
                pe.wait_ge(pT_ready, ONE + n + 1)
                if u == 0:
                    pe.wait_ge(v_ready, ONE + r + 1)
                    pe.wait_ge(at_ready, ONE + r)
                j, half = u // 2, u % 2
                for i in range(UH):
                    g = UH * half + i
                    done = nc.tensor.matmul(bank[4][:, j * P:(j + 1) * P], vz[:, g * P:(g + 1) * P],
                                            probsT[:, u % 2, i, :], start=(g == 0), stop=(g == NG - 1))
                done.then_inc(av_done, 1)
                if not last or u + 2 < NU:
                    pe.wait_ge(masked, ONE + 2 * n + 2)
                    if u == 6:
                        wait_for_row(r + 1)
                    scores((u + 2) % NU)
                if u == 7:
                    pe.wait_ge(wo1_in, 16 * NG)
                    pe.wait_ge(at_ready, ONE + r + 1)
                    if last:
                        pe.wait_ge(xn2T_ls, 5)
                    for j in range(GH):
                        done = nc.tensor.matmul(bank[7][:], atT[:, j, :], wo1[:, j, :], start=(j == 0),
                                                stop=(j == GH - 1))
                    done.then_inc(o_ps, 1)

            pe.wait_ge(ident_in, 16)
            turn_context(0)
            turn_x(0, 0)
            wait_for_split(pe, 2)
            make_q(0)
            wait_for_split(pe, SELF_W)
            make_kv(0)
            turn_k(0)
            turn_q(0)
            wait_for_row(0)
            for u in range(2):
                scores(u)
            wait_for_split(pe, KEY_W)
            self_slot(0, 0, False)
            with pe.Fori(0, NB - 1) as r:
                for u in range(1, NU):
                    self_slot(r, u, False)
                self_slot(r + 1, 0, False)
            def turn_xn2(b):
                if 0 < b < 5:
                    pe.wait_ge(xn2T_ls, b)
                if b == 5:
                    pe.wait_ge(tab_ready, NB // 2)
                if b == NB - 1:
                    pe.wait_ge(xn2T_ls, 6)
                pe.wait_ge(xn2_ready, b + 1)
                transpose_chunks(bank[TURN_BANK[b]], xn2[:, b % 2]).then_inc(xn2T_ps, 1)

            def turn_tables(a, z):
                if a:
                    pe.wait_ge(tab_ready, a // 2)
                else:
                    pe.wait_ge(kxab_done, ONE + 2 * NB)
                for i in range(2):
                    for b in range(a, z):
                        k = 2 * i + b - a
                        last = nc.tensor.transpose(bank[6][:, k * P:(k + 1) * P], rope_x[:, b, i * P:(i + 1) * P],
                                                   ident[:])
                last.then_inc(tab_ps, 1)

            def last_row_fill(u):
                if u in TURN_ROW:
                    turn_xn2(TURN_ROW[u])
                if u in TABLE_ROWS:
                    if u == 6:
                        pe.wait_ge(kxT_ready, ONE + 2 * NB)
                    turn_tables(*TABLE_ROWS[u])
                if u == 7:
                    pe.wait_ge(vx_ready, ONE + 2 * NB)
                    turn_xn2(6)

            for u in range(1, NU):
                self_slot(NB - 1, u, True, last_row_fill)

            pe.wait_ge(x1_ready, ONE + NB)
            pe.wait_ge(tab_ready, NB // 2)
            pe.wait_ge(xn2T_ls, NB // 2)

            def make_piece(m, g, half, head, i, rotated, part=range(EC)):
                pe.wait_ge(ring_l, ONE + g * 8 + head + 1)
                pe.wait_ge(rope_ab, ONE + rotated)
                t = slice(half * HALF_TOK, (half + 1) * HALF_TOK)
                last = product3(bank[i][:], [(wq_h[:, head, c, :], wq_l[:, head, c, :], xn2T_h[:, c, t],
                                              xn2T_l[:, c, t]) for c in part],
                                first=(part[0] == 0), final=(part[-1] == EC - 1))
                if part[-1] == EC - 1:
                    last.then_inc(qp_done, 1)

            def cross_scores(n, g, b, i):
                pe.wait_ge(masked, ONE + 2 * n - 2)
                pe.wait_ge(kv_in, 32 * (g + 1))
                pe.wait_ge(q_ready, ONE + g * 8 + (b // 4) * 4 + 4)
                for h in range(GH):
                    last = nc.tensor.matmul(bank[2 + b % 2][:, h * P:(h + 1) * P], Q[:, h, b * P:(b + 1) * P],
                                            k_g[:, i, b * P:(b + 1) * P], start=True, stop=True)
                last.then_inc(s_ready, 1)

            for m in range(LEAD):
                if m == 3:
                    turn_xn2(NB - 1)
                if m == GH:
                    pe.wait_ge(xn2T_ls, NB)
                make_piece(m, 0, *PIECES[m], m % 2, max(m - 1, 0))
                if m in (4, 5):
                    cross_scores(CROSS0 + m - 4, 0, m - 4, 0)

            def turn_rows(k):
                for b in range(*BATCHES[k]):
                    pe.wait_ge(xn3_ready, b + 1)
                    if b >= 2:
                        pe.wait_ge(xn3T_ready, b - 1)
                    transpose_chunks(bank[b % 2], xn3[:, b, :]).then_inc(xn3T_ps, 1)

            def logits(k):
                if k:
                    pe.wait_ge(lsh_ready, k)
                for b in range(*BATCHES[k]):
                    pe.wait_ge(xn3T_ready, b + 1)
                    last = product(bank[5][:, b * NE:(b + 1) * NE], lambda c: xn3T[:, c, b * P:(b + 1) * P],
                                   lambda c: rwT[:, c, :])
                last.then_inc(lg_ps, 1)

            def turn_weights(k):
                a, z = BATCHES[k]
                pe.wait_ge(wd_ready, k + 1)
                if k:
                    pe.wait_ge(wdT_ready, k)
                for b in range(a, z):
                    last = nc.tensor.transpose(bank[4][0:NE, (b - a) * P:(b - a + 1) * P], wd[:, b, :], ident[:])
                last.then_inc(wdT_ps, 1)

            def place_residual(b):
                nc.tensor.matmul(bank[MIX_BANK[b]][:], ident[:], X[:, b, :], start=True, stop=False)

            def mix(k):
                pe.wait_ge(wdT_ready, k + 1)
                for b in range(*BATCHES[k]):
                    if b in (3, 4, 5):
                        pe.wait_ge(fin_ready, b - 2)
                    nc.tensor.matmul(bank[MIX_BANK[b]][:], wdT[:, b * P:(b + 1) * P], eb[:], start=(k < 2),
                                     stop=True).then_inc(mix_ps, 1)

            def cross_output(g, i, b):
                pe.wait_ge(ring_l, ONE + (g + 1) * 8)
                pe.wait_ge(oT_hs, ONE + g * NU + b + 1)
                pe.wait_ge(acc_done, ONE + g * NU + b)
                for h in range(GH):
                    nc.tensor.matmul(bank[7][:], oT_h[:, h, :], wo_l[:, i, h, :], start=(h == 0), stop=False)
                    nc.tensor.matmul(bank[7][:], oT_h[:, h, :], wo_h[:, i, h, :], start=False, stop=False)
                pe.wait_ge(oT_ls, ONE + g * NU + b + 1)
                for h in range(GH):
                    last = nc.tensor.matmul(bank[7][:], oT_l[:, h, :], wo_h[:, i, h, :], start=False,
                                            stop=(h == GH - 1))
                last.then_inc(y_done, 1)

            def group(g, i, last_group):
                for b in range(NB):
                    n = CROSS0 + g * NU + b
                    pe.wait_ge(pT_ready, ONE + n)
                    transpose_probs(b % 2, n, bank[4])
                    if b + 2 < NB:
                        cross_scores(n + 2, g, b + 2, i)
                    elif not last_group:
                        cross_scores(n + 2, g + 1, b + 2 - NB, 1 - i)
                    if last_group and b:
                        cross_output(g, i, b - 1)
                    ahead, k = piece_at(b)
                    made = not (ahead and last_group)
                    m = g * 8 + LEAD + b
                    if made:
                        half, head = PIECES[k]
                        make_piece(m, g + ahead, half, head, (LEAD + b) % 2, m - 1, range(0, 1))
                    pe.wait_ge(pT_ready, ONE + n + 1)
                    pe.wait_ge(v_ls, ONE + g + 1)
                    pe.wait_ge(oT_ls, ONE + g * NU + b)
                    nc.tensor.matmul(bank[6][:], v_h[:, i, b, :], pT_h[:], start=True, stop=False)
                    nc.tensor.matmul(bank[6][:], v_l[:, i, b, :], pT_h[:], start=False, stop=False)
                    pe.wait_ge(pT_ls, ONE + (n - CROSS0) + 1)
                    nc.tensor.matmul(bank[6][:], v_h[:, i, b, :], pT_l[:], start=False, stop=True)\
                        .then_inc(av_done, 1)
                    if made:
                        make_piece(m, g + ahead, half, head, (LEAD + b) % 2, m - 1, range(1, EC))
                    if last_group and b == 2:
                        pe.wait_ge(ffn_in, 48)
                        for c in range(EC):
                            last = nc.tensor.transpose(bank[5][:, c * NE:(c + 1) * NE], rw[:, c * P:(c + 1) * P],
                                                       ident[0:NE, 0:NE])
                        last.then_inc(rwT_ps, 1)
                    if last_group and b == 4:
                        turn_rows(0)
                    if last_group and b == 5:
                        pe.wait_ge(rwT_ready, 1)
                        logits(0)
                    if last_group and b == 7:
                        turn_rows(1)
                        logits(1)
                    if not last_group:
                        cross_output(g, i, b)

            with pe.Fori(0, NG // 2 - 1) as g2:
                for i in range(2):
                    group(g2 * 2 + i, i, False)
            group(NG - 2, 0, False)
            group(NG - 1, 1, True)

            cross_output(NG - 1, 1, NB - 1)
            turn_weights(0)
            pe.wait_ge(rest_zero, 2)
            mix(0)
            pe.wait_ge(acc_done, ONE + NG * NU)
            place_residual(6)
            turn_rows(2)
            turn_weights(1)
            logits(2)
            place_residual(7)
            mix(1)
            turn_weights(2)
            mix(2)


def constants():
    import numpy as np

    f = np.float32
    steps = np.arange(P, dtype=f)
    inv = (f(1) / f(500000.0) ** (np.arange(0, SD, 2, dtype=f) / f(SD))).astype(f)
    angle = (steps[:, None] * inv[None, :]).astype(f)
    c, s = np.cos(angle), np.sin(angle)
    rope_self = np.concatenate([c, c, -s, s], 1).astype(f)
    inv = (f(1) / f(10000.0) ** (np.arange(0, XD, 2, dtype=f) / f(XD))).astype(f)
    angle = (np.arange(MAXPOS, dtype=f)[:, None] * inv[None, :]).astype(f)
    c, s = np.cos(angle), np.sin(angle)
    rope_cross = np.concatenate([c, c, s, -s], 1).astype(f)
    causal = np.where(np.triu(np.ones((P, P), bool), 1), f(NEG), f(0)).astype(f)
    rows = (np.arange(P)[:, None] // SD == np.arange(NG)[None, :]).astype(f)
    return {"c_ident": np.eye(P, dtype=f), "c_causal": causal, "c_rope_self": rope_self,
            "c_rope_cross": rope_cross, "c_rows": rows}


_INS = ["x", "ctx_4096", "pos_BxS2", "mask_BxSxS2_ik0", "L0_attn_Wq", "L0_attn_Wk", "L0_attn_Wv", "L0_attn_Wo",
        "L0_xattn_Wq", "L0_xattn_Wk", "L0_xattn_Wv", "L0_xattn_Wo", "L0_ffn_router_weight", "L0_ffn_router_bias",
        "L0_ffn_expert_bias"]


def kernel(**inputs):
    import numpy as _np
    import concourse.bacc as _bacc
    from concourse import mybir as _mybir
    from concourse.bass_utils import run_bass_kernel_spmd as _run

    nc = _bacc.Bacc("TRN2", target_bir_lowering=False, num_devices=1)
    arrays, args = {}, []
    for name, a in [(n, inputs[n]) for n in _INS] + list(constants().items()):
        a = _np.ascontiguousarray(_np.transpose(a) if name == "pos_BxS2" else a)
        arrays[f"in_{name}"] = a
        args.append(nc.dram_tensor(f"in_{name}", a.shape, _mybir.dt.from_np(a.dtype), kind="ExternalInput").ap())
    args.append(nc.dram_tensor("out_0", (NB, P, E), F32, kind="ExternalOutput").ap())
    decoder(nc, *args)
    r = _run(nc, [arrays], core_ids=[0])
    return r.results[0]["out_0"]
```
